# Optimizing a Trainium2 kernel written in Bass

```python
import numpy as np
import jax
import jax.numpy as jnp

def _softmax(x, axis=-1):
    return jax.nn.softmax(x, axis=axis)

def _gelu(x):
    return jax.nn.gelu(x, approximate=True)

def _silu(x):
    return jax.nn.silu(x)

def _sigmoid(x):
    return jax.nn.sigmoid(x)

def _layernorm(x, axis=-1, eps=1e-05):
    m = jnp.mean(x, axis=axis, keepdims=True)
    v = jnp.var(x, axis=axis, keepdims=True)
    return (x - m) / jnp.sqrt(v + eps)

def _scatter_add(tgt, idx, src, axis=0):
    return tgt.at[idx].add(src)

def _segment_sum(src, seg, n):
    return jax.ops.segment_sum(src, seg, n)
kernel_name = 'mk_seq_preln_d1_jaxref_r8_94be7d'

def setup_inputs(seed: int=0):
    np.random.seed(seed)
    _w = jnp.asarray

    def _L0_attn_setup():
        import jax, jax.numpy as jnp
        import numpy as np
        D_MODEL = 128
        NUM_HEADS = 16
        DEPTH = D_MODEL // NUM_HEADS

        def _split_heads(t, B, S):
            return t.reshape(B, S, NUM_HEADS, DEPTH).transpose(0, 2, 1, 3)
        key = jax.random.key(seed)
        ks = jax.random.split(key, 5)
        B, S = (2, 256)
        scale = 1.0 / np.sqrt(D_MODEL)
        return {'x': jax.random.normal(ks[0], (B, S, D_MODEL), dtype=jnp.float32), 'wq': jax.random.normal(ks[1], (D_MODEL, D_MODEL), dtype=jnp.float32) * scale, 'wk': jax.random.normal(ks[2], (D_MODEL, D_MODEL), dtype=jnp.float32) * scale, 'wv': jax.random.normal(ks[3], (D_MODEL, D_MODEL), dtype=jnp.float32) * scale, 'wo': jax.random.normal(ks[4], (D_MODEL, D_MODEL), dtype=jnp.float32) * scale, 'bo': jnp.zeros((D_MODEL,), dtype=jnp.float32)}
    _L0_attn_in = _L0_attn_setup()

    def _L0_ffn_setup():
        import jax, jax.numpy as jnp
        import numpy as np
        TOP_K = 2

        def _mlp(x, w_fc, w_proj):
            return jnp.square(jax.nn.relu(x @ w_fc.T)) @ w_proj.T
        key = jax.random.key(seed)
        ks = jax.random.split(key, 6)
        B, S, D, E = (4, 256, 128, 8)
        d_ff = 4 * D
        x = jax.random.normal(ks[0], (B, S, D), dtype=jnp.float32)
        router_w = jax.random.normal(ks[1], (E, D), dtype=jnp.float32) * 0.02
        w_fc = jax.random.normal(ks[2], (E, d_ff, D), dtype=jnp.float32) * 0.02
        w_proj = jax.random.normal(ks[3], (E, D, d_ff), dtype=jnp.float32) * 0.02
        shared_fc = jax.random.normal(ks[4], (d_ff, D), dtype=jnp.float32) * 0.02
        shared_proj = jax.random.normal(ks[5], (D, d_ff), dtype=jnp.float32) * 0.02
        return {'x': x, 'router_w': router_w, 'w_fc': w_fc, 'w_proj': w_proj, 'shared_fc': shared_fc, 'shared_proj': shared_proj}
    _L0_ffn_in = _L0_ffn_setup()
    _d = {'L0_attn_x': _L0_attn_in['x'], 'L0_attn_wq': _L0_attn_in['wq'], 'L0_attn_wk': _L0_attn_in['wk'], 'L0_attn_wv': _L0_attn_in['wv'], 'L0_attn_wo': _L0_attn_in['wo'], 'L0_attn_bo': _L0_attn_in['bo'], 'L0_ffn_router_w': _L0_ffn_in['router_w'], 'L0_ffn_w_fc': _L0_ffn_in['w_fc'], 'L0_ffn_w_proj': _L0_ffn_in['w_proj'], 'L0_ffn_shared_fc': _L0_ffn_in['shared_fc'], 'L0_ffn_shared_proj': _L0_ffn_in['shared_proj']}
    _x0 = _d['L0_attn_x']
    _d['L0_attn_x'] = jax.random.normal(jax.random.fold_in(jax.random.key(seed), 1), (32, 256, 128), dtype=_x0.dtype)
    del _x0
    return _d

def reference(L0_attn_x, L0_attn_wq, L0_attn_wk, L0_attn_wv, L0_attn_wo, L0_attn_bo, L0_ffn_router_w, L0_ffn_w_fc, L0_ffn_w_proj, L0_ffn_shared_fc, L0_ffn_shared_proj):

    def _L0_attn_ref(x, wq, wk, wv, wo, bo):
        import jax, jax.numpy as jnp
        import numpy as np
        D_MODEL = 128
        NUM_HEADS = 16
        DEPTH = D_MODEL // NUM_HEADS

        def _split_heads(t, B, S):
            return t.reshape(B, S, NUM_HEADS, DEPTH).transpose(0, 2, 1, 3)
        B, S, _ = x.shape
        q = _split_heads(x @ wq, B, S)
        k = _split_heads(x @ wk, B, S)
        v = _split_heads(x @ wv, B, S)
        scores = jnp.einsum('bhqd,bhkd->bhqk', q, k) / jnp.sqrt(jnp.float32(DEPTH))
        weights = jax.nn.softmax(scores, axis=-1)
        attn = jnp.einsum('bhqk,bhkd->bhqd', weights, v)
        concat = attn.transpose(0, 2, 1, 3).reshape(B, S, D_MODEL)
        return concat @ wo + bo

    def _L0_ffn_ref(x, router_w, w_fc, w_proj, shared_fc, shared_proj):
        import jax, jax.numpy as jnp
        import numpy as np
        TOP_K = 2

        def _mlp(x, w_fc, w_proj):
            return jnp.square(jax.nn.relu(x @ w_fc.T)) @ w_proj.T
        B, S, D = x.shape
        E = router_w.shape[0]
        T = B * S
        flat = x.reshape(T, D)
        logits = flat @ router_w.T
        probs = jax.nn.softmax(logits.astype(jnp.float32), axis=-1)
        topk_p, topk_i = jax.lax.top_k(probs, TOP_K)
        topk_w = (topk_p / jnp.maximum(topk_p.sum(-1, keepdims=True), 1e-09)).astype(flat.dtype)
        combine = jnp.zeros((T, E), dtype=flat.dtype)
        combine = combine.at[jnp.arange(T)[:, None], topk_i].add(topk_w)
        out = jnp.zeros_like(flat)
        for e in range(E):
            out = out + _mlp(flat, w_fc[e], w_proj[e]) * combine[:, e:e + 1]
        out = out + _mlp(flat, shared_fc, shared_proj)
        return out.reshape(B, S, D)
    x = L0_attn_x
    x = x + _L0_attn_ref(_layernorm(x, axis=-1), L0_attn_wq, L0_attn_wk, L0_attn_wv, L0_attn_wo, L0_attn_bo)
    x = x + _L0_ffn_ref(_layernorm(x, axis=-1), L0_ffn_router_w, L0_ffn_w_fc, L0_ffn_w_proj, L0_ffn_shared_fc, L0_ffn_shared_proj)
    return x

_drawn_inputs = setup_inputs


def setup_inputs(seed=0):
    import zlib

    import numpy as np

    out = dict(_drawn_inputs(seed))
    spreads = {'L0_attn_bo': (0.0, 0.1)}
    factors = {'L0_ffn_router_w': 3.234, 'L0_ffn_w_fc': 3.116, 'L0_ffn_w_proj': 2.854}
    for name, (base, spread) in spreads.items():
        noise = np.random.default_rng([zlib.crc32(name.encode()), seed]).standard_normal(out[name].shape)
        drawn = base * np.exp(spread * noise) if base else spread * noise
        out[name] = jnp.asarray(drawn.astype(out[name].dtype))
    for name, factor in factors.items():
        out[name] = (out[name] * factor).astype(out[name].dtype)
    return out
```

```python
import concourse.bass as bass
from concourse import mybir
from contextlib import ExitStack

F32 = mybir.dt.float32
BF16 = mybir.dt.bfloat16
ALU = mybir.AluOpType
ACT = mybir.ActivationFunctionType
AX = mybir.AxisListType

P = 128
EPS = 1e-5
U = 4


class Batch:

    def __init__(self, i, c, total):
        self.i, self.c, self.total = i, c, total

    def __add__(self, n):
        return Batch(self.i, self.c + n, self.total)

    def __sub__(self, n):
        return self + (-n)

    @property
    def on(self):
        return self.i is not None or 0 <= self.c < self.total

    def mod(self, m):
        return self.c % m

    def times(self, k, n=0):
        return k * self.c + n if self.i is None else self.i * (k * U) + (k * self.c + n)

    def turn(self, m, k, n=0):
        return k * (self.c // m) + n if self.i is None else self.i * (k * (U // m)) + (k * (self.c // m) + n)


def wait(eng, sem, value):
    if isinstance(value, int) and value <= 0:
        return
    eng.wait_ge(sem, value)


SHARED_USES = [("xnT", 1), ("v", 1), ("mT", -1), ("xn2T", -4), ("concT", -3), ("wo", -3)]


def shared_use(t, name):
    at = [n for n, _ in SHARED_USES].index(name)

    def before(step, upto):
        return sum(0 <= s + d < t.total for s in range(-U, step) for _, d in SHARED_USES) + sum(
            0 <= step + d < t.total for _, d in SHARED_USES[:upto])

    if t.i is None:
        return before(t.c, at)
    return t.i * (U * len(SHARED_USES)) + (before(U, 0) + (t.c - U) * len(SHARED_USES) + at)


def shared_after(t, name):
    return shared_use(t, name) + 1


def attention(nc, x, wq, wk, wv, wo, bo, x1_all, xn2T_all):
    B, S, D = x.shape
    H = 16
    DH = D // H
    QB = S // P
    G = H // 4
    VW = 32
    PARTS = 3
    KR = PARTS * PARTS * DH
    KS = 96
    KM = KS + PARTS
    SCALE = float(DH) ** -0.5
    NT = B * QB
    FIRST, LOOPED = -2, U
    TURNS = (B - 3 - U) // U
    LAST = B + 4
    STORED = 16 * (1 + PARTS)
    STACKED = 16 * (PARTS + 1)

    with ExitStack() as ctx:
        def sb(name, shape, dt=F32):
            return ctx.enter_context(nc.sbuf_tensor(name, shape, dt))

        def ps(name, shape):
            return ctx.enter_context(nc.psum_tensor(name, shape, F32))

        def sem(name):
            return ctx.enter_context(nc.semaphore(name))

        ident = sb("ident", [P, P])
        minus_half = sb("minus_half", [P, QB])
        eps_sb = sb("eps_sb", [P, QB])
        wq_sb, wk_sb, wv_sb, wo_sb = (sb(n, [D, D]) for n in ("wq_sb", "wk_sb", "wv_sb", "wo_sb"))
        bo_sb = sb("bo_sb", [P, D])
        x_in = sb("x_in", [P, 2, QB, D])
        stats1 = sb("stats1", [P, QB, 6])
        mv1 = sb("mv1", [P, 2, QB, 2])
        centred1 = sb("centred1", [P, QB, D])
        rstd1 = sb("rstd1", [P, QB])
        xn1 = sb("xn1", [P, 2, QB, D])
        xnT = sb("xnT", [D, S])
        qk_parts = sb("qk_parts", [P, 2, PARTS, 2, S], BF16)
        qk_rest = sb("qk_rest", [P, 2, S])
        q_stack = sb("q_stack", [KM, U, H, S], BF16)
        k_stack = sb("k_stack", [KM, U, H, S], BF16)
        filler = sb("filler", [P, 2, P], BF16)
        ident_bf = sb("ident_bf", [P, P], BF16)
        v_aug = sb("v_aug", [P, U, QB, H, VW])
        neg_max = sb("neg_max", [P, 2, QB, H])
        m_parts = sb("m_parts", [P, QB, P // H, H], BF16)
        m_rest = sb("m_rest", [P, QB, H])
        mT = sb("mT", [PARTS * H, S], BF16)
        probs = sb("probs", [P, 8, QB, S])
        o_sb = sb("o_sb", [P, 2, G, S])
        rden = sb("rden", [P, H])
        conc = sb("conc", [P, QB, H, DH])
        concT = sb("concT", [D, S])
        x_res = sb("x_res", [P, 2, QB, D])
        xb = sb("xb", [P, QB, D])
        x1 = sb("x1", [P, 2, QB, D])
        stats2 = sb("stats2", [P, QB, 6])
        mv2 = sb("mv2", [P, 2, QB, 2])
        centred2 = sb("centred2", [P, QB, D])
        rstd2 = sb("rstd2", [P, QB])
        xn2 = sb("xn2", [P, QB, D])

        q_dram = nc.dram_tensor("q_parts", (2, PARTS, DH, H, S), BF16, kind="Internal").ap()
        k_dram = nc.dram_tensor("k_parts", (2, PARTS, PARTS, DH, H, S), BF16, kind="Internal").ap()

        ps_s = [ps(f"ps_s{n}", [P, QB, S]) for n in range(2)]
        ps_st = [ps(f"ps_st{n}", [P, QB, S]) for n in range(2)]
        ps_o = ps("ps_o", [P, 512])
        ps_qk = ps("ps_qk", [P, 2, S])
        ps_ot = ps("ps_ot", [P, G, P])
        ps_shared = ps("ps_shared", [P, 512])
        ps_shared_bf = ps_shared[:, :].bitcast(BF16)

        consts_loaded = sem("consts_loaded")
        consts_ready = sem("consts_ready")
        half_ready = sem("half_ready")
        vpad_ready = sem("vpad_ready")
        rows_filled = sem("rows_filled")
        x_loaded = [sem(f"x_loaded{n}") for n in range(2)]
        stats1_done = sem("stats1_done")
        mv1_ready = sem("mv1_ready")
        rstd1_steps = sem("rstd1_steps")
        xn1_ready = sem("xn1_ready")
        xnT_done = sem("xnT_done")
        qk_done = sem("qk_done")
        qk_hi_ready = sem("qk_hi_ready")
        qk_rest_ready = sem("qk_rest_ready")
        qk_mid_ready = sem("qk_mid_ready")
        qk_lo_ready = sem("qk_lo_ready")
        parts_stored = [sem(f"parts_stored{n}") for n in range(2)]
        v_done = sem("v_done")
        stacked = [sem(f"stacked{n}") for n in range(2)]
        scores_done = sem("scores_done")
        max_done = sem("max_done")
        m_hi_ready = sem("m_hi_ready")
        m_rest_ready = sem("m_rest_ready")
        m_mid_ready = sem("m_mid_ready")
        m_lo_ready = sem("m_lo_ready")
        mT_done = sem("mT_done")
        m_stacked = [sem(f"m_stacked{n}") for n in range(2)]
        scoresT_done = sem("scoresT_done")
        exp_done = sem("exp_done")
        pv_done = sem("pv_done")
        o_ready = sem("o_ready")
        ot_done = sem("ot_done")
        rden_ready = sem("rden_ready")
        conc_ready = sem("conc_ready")
        concT_done = sem("concT_done")
        wo_done = sem("wo_done")
        xres_loaded = [sem(f"xres_loaded{n}") for n in range(2)]
        xb_ready = sem("xb_ready")
        x1_kept = sem("x1_kept")
        stats2_done = sem("stats2_done")
        mv2_ready = sem("mv2_ready")
        rstd2_steps = sem("rstd2_steps")
        xn2_ready = sem("xn2_ready")
        xn2T_done = sem("xn2T_done")
        shared_free = sem("shared_free")

        x_v = x.rearrange("b (q p) d -> p b q d", p=P)
        x_rows = x.rearrange("b s d -> (b s) d")

        def x_batch(row):
            rows = x_rows[bass.ds(row, S), :]
            return rows.rearrange("(q p) d -> p q d", p=P)

        def steps(eng, step):
            for c in range(FIRST, LOOPED):
                step(Batch(None, c, B))
            with eng.Fori(0, TURNS) as i:
                for c in range(LOOPED, LOOPED + U):
                    step(Batch(i, c, B))
            for c in range(LOOPED + U * TURNS, LAST + 1):
                step(Batch(None, c, B))

        block = ctx.enter_context(nc.Block())

        @block.sync
        def _(sp):
            for w, src in ((wq_sb, wq), (wk_sb, wk), (wv_sb, wv), (wo_sb, wo)):
                sp.dma_start(w[:, :], src).then_inc(consts_loaded, 16)
            sp.dma_start(bo_sb[:, :], bo.rearrange("(a n) -> a n", a=1).broadcast_to([P, D])).then_inc(consts_loaded, 16)

            sp.wait_ge(consts_ready, 5)
            for n in range(U):
                for stack in (q_stack, k_stack):
                    sp.dma_start(stack[KR:KS, n, :, :].rearrange("p h t -> p (h t)"),
                                 filler[:, 0:1, :].broadcast_to([P, (KS - KR) * H * S // P // P, P])
                                 ).then_inc(rows_filled, 16)
                sp.dma_start(k_stack[KS:KM, n, :, :].rearrange("p h t -> p (h t)"),
                             filler[0:96, 1:2, :].broadcast_to([96, PARTS * H * S // P // 96, P])
                             ).then_inc(rows_filled, 16)

            def step(t):
                b = t + 3
                if t.c == FIRST and t.i is None:
                    sp.dma_start(x_in[:, 0, :, :], x_batch(0)).then_inc(x_loaded[0], 16)
                if b.on:
                    wait(sp, xn1_ready, b.times(1, -1))
                    sp.dma_start(x_in[:, b.mod(2), :, :], x_batch(b.times(S))).then_inc(x_loaded[b.mod(2)], 16)
                b = t - 2
                if b.on:
                    wait(sp, xb_ready, b.times(1, -1))
                    sp.dma_start(x_res[:, b.mod(2), :, :], x_batch(b.times(S))).then_inc(xres_loaded[b.mod(2)], 16)
                b = t + 1
                if b.on:
                    wait(sp, qk_lo_ready, b.times(1, 1))
                    part = qk_parts[:, b.mod(2), :, :, :]
                    sp.dma_start(q_dram[b.mod(2)].rearrange("i d h t -> (d h) i t"),
                                 part[:, :, 0, :]).then_inc(parts_stored[b.mod(2)], 16)
                    for i in range(PARTS):
                        sp.dma_start(k_dram[b.mod(2), :, i].rearrange("j d h t -> (d h) j t"),
                                     part[:, :, 1, :]).then_inc(parts_stored[b.mod(2)], 16)
                b = t - 1
                if b.on:
                    wait(sp, shared_free, shared_after(t, "mT"))
                    sp.dma_start(q_stack[KS:KM, b.mod(U), :, :], mT[:, :]).then_inc(m_stacked[b.mod(2)], 16)
                b = t + 1
                if b.on:
                    wait(sp, parts_stored[b.mod(2)], b.turn(2, STORED, STORED))
                    for j in range(PARTS):
                        at = j * PARTS * DH
                        sp.dma_start(q_stack[at:at + PARTS * DH, b.mod(U), :, :],
                                     q_dram[b.mod(2)].rearrange("i d h t -> (i d) h t")
                                     ).then_inc(stacked[b.mod(2)], 16)
                    sp.dma_start(k_stack[0:KR, b.mod(U), :, :],
                                 k_dram[b.mod(2)].rearrange("j i d h t -> (j i d) h t")
                                 ).then_inc(stacked[b.mod(2)], 16)

            steps(sp, step)
        @block.gpsimd
        def _(pool):
            pool.memset(ident[:, :], 0.0).then_inc(consts_ready, 1)
            pool.wait_ge(consts_ready, 1)
            pool.affine_select(out=ident[:, :], in_=ident[:, :], compare_op=ALU.not_equal, fill=1.0, base=0,
                               pattern=[[-1, P]], channel_multiplier=1).then_inc(consts_ready, 1)
            pool.wait_ge(consts_ready, 2)
            pool.memset(filler[:, 0, :], 0.0).then_inc(consts_ready, 1)
            pool.memset(filler[:, 1, :], 1.0).then_inc(consts_ready, 1)
            pool.tensor_copy(ident_bf[:, :], ident[:, :]).then_inc(consts_ready, 1)
            pool.memset(minus_half[:, :], -0.5).then_inc(half_ready, 1)
            pool.memset(eps_sb[:, :], EPS).then_inc(half_ready, 1)
            pool.wait_ge(half_ready, 2)
            pool.wait_ge(consts_loaded, 16 * 5)

            def normalise(mv, centred, rs, out_, src, chain, b):
                pool.tensor_tensor(rs[:, :], mv[:, b.mod(2), :, 1], eps_sb[:, :], ALU.add).then_inc(chain, 1)
                pool.tensor_tensor(centred[:, :, :], src,
                                   mv[:, b.mod(2), :, 0:1].broadcast_to([P, QB, D]), ALU.subtract).then_inc(chain, 1)
                wait(pool, chain, b.times(3, 1))
                pool.tensor_tensor(rs[:, :], rs[:, :], minus_half[:, :], ALU.pow).then_inc(chain, 1)
                wait(pool, chain, b.times(3, 3))
                return pool.tensor_tensor(out_, centred[:, :, :], rs[:, :].unsqueeze(2).broadcast_to([P, QB, D]),
                                          ALU.mult)

            def step(t):
                b = t + 1
                if b.on:
                    wait(pool, qk_mid_ready, b.times(1, 1))
                    pool.tensor_tensor(qk_parts[:, b.mod(2), 2, :, :], qk_rest[:, :, :],
                                       qk_parts[:, b.mod(2), 1, :, :], ALU.subtract).then_inc(qk_lo_ready, 1)
                b = t + 2
                if b.on:
                    wait(pool, mv1_ready, b.times(1, 1))
                    wait(pool, xn1_ready, b.times(1))
                    wait(pool, xnT_done, b.times(1, -1))
                    normalise(mv1, centred1, rstd1, xn1[:, b.mod(2), :, :], x_in[:, b.mod(2), :, :],
                              rstd1_steps, b).then_inc(xn1_ready, 1)
                b = t - 3
                if b.on:
                    wait(pool, xres_loaded[b.mod(2)], b.turn(2, 16, 16))
                    wait(pool, x1_kept, b.times(1))
                    for q in range(QB):
                        last = pool.tensor_tensor(xb[:, q, :], x_res[:, b.mod(2), q, :], bo_sb[:, :], ALU.add)
                    last.then_inc(xb_ready, 1)
                    wait(pool, mv2_ready, b.times(1, 1))
                    wait(pool, xn2_ready, b.times(1))
                    wait(pool, xn2T_done, b.times(1))
                    normalise(mv2, centred2, rstd2, xn2[:, :, :], x1[:, b.mod(2), :, :],
                              rstd2_steps, b).then_inc(xn2_ready, 1)

            steps(pool, step)

        @block.tensor
        def _(pe):
            pe.wait_ge(consts_ready, 5)
            pe.wait_ge(consts_loaded, 16 * 5)
            pe.wait_ge(vpad_ready, 2)
            pe.wait_ge(rows_filled, 16 * 3 * U)

            def xnT_use(t):
                b = t + 1
                wait(pe, shared_free, shared_use(t, "xnT"))
                wait(pe, xn1_ready, b.times(1, 1))
                for q in range(QB):
                    last = pe.transpose(ps_shared[:, q * P:(q + 1) * P], xn1[:, b.mod(2), q, :], ident[:, :])
                last.then_inc(xnT_done, 1)

            def project_qk(t):
                b = t + 1
                wait(pe, shared_free, shared_after(t, "xnT"))
                wait(pe, qk_rest_ready, b.times(1))
                pe.matmul(ps_qk[:, 0, :], wq_sb[:, :], xnT[:, :], start=True, stop=True)
                pe.matmul(ps_qk[:, 1, :], wk_sb[:, :], xnT[:, :], start=True, stop=True,
                          skip_group_check=True).then_inc(qk_done, 1)

            def project_v(t):
                for q in range(QB):
                    last = pe.matmul(ps_shared[:, q * D:(q + 1) * D], xnT[:, q * P:(q + 1) * P], wv_sb[:, :],
                                     start=True, stop=True, skip_group_check=True)
                last.then_inc(v_done, 1)

            def scores(b, h):
                if h == 0:
                    wait(pe, stacked[b.mod(2)], b.turn(2, STACKED, STACKED))
                wait(pe, max_done, b.times(H, h - 1))
                for q in range(QB):
                    last = pe.matmul(ps_s[h % 2][:, q, :], q_stack[0:KS, b.mod(U), h, q * P:(q + 1) * P],
                                     k_stack[0:KS, b.mod(U), h, :], start=True, stop=True, skip_group_check=True)
                last.then_inc(scores_done, 1)

            def maxT(t):
                b = t - 1
                wait(pe, shared_free, shared_use(t, "mT"))
                wait(pe, m_lo_ready, b.times(1, 1))
                for q in range(QB):
                    last = pe.transpose(ps_shared_bf[:, q * P:(q + 1) * P],
                                        m_parts[:, q, :, :].rearrange("p i h -> p (i h)"), ident_bf[:, :])
                last.then_inc(mT_done, 1)

            def scoresT(b, h):
                if h == 0:
                    wait(pe, m_stacked[b.mod(2)], b.turn(2, 16, 16))
                wait(pe, exp_done, b.times(H, h - 1))
                for k in range(QB):
                    last = pe.matmul(ps_st[h % 2][:, k, :], k_stack[0:KM, b.mod(U), h, k * P:(k + 1) * P],
                                     q_stack[0:KM, b.mod(U), h, :], start=True, stop=True, skip_group_check=True)
                last.then_inc(scoresT_done, 1)

            def pv(b, g):
                wait(pe, exp_done, b.times(H, 4 * g + 4))
                wait(pe, o_ready, b.times(G, g))
                for k in range(QB):
                    for j in range(4):
                        h = 4 * g + j
                        last = pe.matmul(ps_o[32 * j:32 * j + VW, 0:S], v_aug[:, b.mod(U), k, h, :],
                                         probs[:, h % 8, k, :], start=k == 0, stop=k == QB - 1,
                                         skip_group_check=True)
                last.then_inc(pv_done, 1)

            def oT(b, q):
                wait(pe, o_ready, b.times(G, G))
                wait(pe, conc_ready, b.times(QB, q))
                for g in range(G):
                    last = pe.transpose(ps_ot[:, g, :], o_sb[:, b.mod(2), g, q * P:(q + 1) * P], ident[:, :])
                last.then_inc(ot_done, 1)

            def xn2T_use(t):
                b = t - 4
                wait(pe, shared_free, shared_use(t, "xn2T"))
                wait(pe, xn2_ready, b.times(1, 1))
                for q in range(QB):
                    last = pe.transpose(ps_shared[:, q * P:(q + 1) * P], xn2[:, q, :], ident[:, :])
                last.then_inc(xn2T_done, 1)

            def concT_use(t):
                b = t - 3
                wait(pe, shared_free, shared_use(t, "concT"))
                wait(pe, conc_ready, b.times(QB, QB))
                for q in range(QB):
                    last = pe.transpose(ps_shared[:, q * P:(q + 1) * P],
                                        conc[:, q, :, :].rearrange("p h d -> p (h d)"), ident[:, :])
                last.then_inc(concT_done, 1)

            def project_o(t):
                wait(pe, shared_free, shared_after(t, "concT"))
                for q in range(QB):
                    last = pe.matmul(ps_shared[:, q * D:(q + 1) * D], concT[:, q * P:(q + 1) * P], wo_sb[:, :],
                                     start=True, stop=True, skip_group_check=True)
                last.then_inc(wo_done, 1)

            def step(t):
                a, m, c, e, f = t + 1, t - 1, t - 2, t - 3, t - 4
                for h in range(H):
                    if h == 0 and a.on:
                        xnT_use(t)
                    if h == 2 and a.on:
                        project_qk(t)
                    if h == 3 and a.on:
                        wait(pe, shared_free, shared_after(t, "xnT"))
                        project_v(t)
                    if h == 5 and m.on:
                        maxT(t)
                    if h == 8 and f.on:
                        xn2T_use(t)
                    if h == 10 and e.on:
                        concT_use(t)
                    if h == 12 and e.on:
                        project_o(t)
                    if t.on:
                        scores(t, h)
                    if c.on:
                        scoresT(c, h)
                    if h == 1 and e.on:
                        pv(e, G - 1)
                    if h in (5, 9, 13) and c.on:
                        pv(c, h // 4 - 1)
                    if h in (4, 7) and e.on:
                        oT(e, h // 6)

            steps(pe, step)

        @block.scalar
        def _(act):
            def xnT_copy(t):
                b = t + 1
                wait(act, xnT_done, b.times(1, 1))
                wait(act, v_done, b.times(1))
                act.activation(xnT[:, :], ps_shared[:, 0:S], ACT.Copy).then_inc(shared_free, 1)

            def q_hi(t):
                b = t + 1
                wait(act, qk_done, b.times(1, 1))
                wait(act, parts_stored[b.mod(2)], b.turn(2, STORED))
                act.activation(qk_parts[:, b.mod(2), 0, :, :], ps_qk[:, :, :], ACT.Copy).then_inc(qk_hi_ready, 1)

            def v_copy(t):
                b = t + 1
                wait(act, v_done, b.times(1, 1))
                wait(act, pv_done, b.times(G, -(U - 1) * G))
                act.activation(v_aug[:, b.mod(U), :, :, 0:DH],
                               ps_shared[:, 0:QB * D].rearrange("p (q h d) -> p q h d", q=QB, h=H),
                               ACT.Copy).then_inc(shared_free, 1)

            def exp(b, h):
                wait(act, scoresT_done, b.times(H, h + 1))
                if h % 4 == 0:
                    wait(act, pv_done, b.times(G, h // 4 - 1))
                act.activation(probs[:, h % 8, :, :], ps_st[h % 2][:, :, :], ACT.Exp,
                               scale=SCALE).then_inc(exp_done, 1)

            def o_copy(b, g):
                wait(act, pv_done, b.times(G, g + 1))
                if g == 0:
                    wait(act, ot_done, b.times(QB, -QB))
                act.activation(o_sb[:, b.mod(2), g, :], ps_o[:, 0:S], ACT.Copy).then_inc(o_ready, 1)

            def xn2T_copy(t):
                b = t - 4
                wait(act, xn2T_done, b.times(1, 1))
                act.activation(xn2T_all[:, bass.ds(b.times(S), S)], ps_shared[:, 0:S], ACT.Copy).then_inc(shared_free, 1)

            def concT_copy(t):
                b = t - 3
                wait(act, concT_done, b.times(1, 1))
                act.activation(concT[:, :], ps_shared[:, 0:S], ACT.Copy).then_inc(shared_free, 1)

            def step(t):
                a, c, e, f = t + 1, t - 2, t - 3, t - 4
                for h in range(H):
                    if c.on:
                        exp(c, h)
                    if h == 0 and a.on:
                        xnT_copy(t)
                    if h == 2 and e.on:
                        o_copy(e, G - 1)
                    if h == 3 and a.on:
                        q_hi(t)
                    if h == 4 and a.on:
                        v_copy(t)
                    if h in (6, 10, 14) and c.on:
                        o_copy(c, h // 4 - 1)
                    if h == 9 and f.on:
                        xn2T_copy(t)
                    if h == 11 and e.on:
                        concT_copy(t)

            steps(act, step)

        @block.vector
        def _(dve):
            dve.memset(m_parts[:, :, PARTS:P // H, :], 0.0)
            dve.memset(v_aug[:, :, :, :, DH:VW], 0.0).then_inc(vpad_ready, 1)
            dve.wait_ge(vpad_ready, 1)
            dve.memset(v_aug[:, :, :, :, DH:DH + 1], 1.0).then_inc(vpad_ready, 1)

            def norm_stats(src, stats, stats_done, b):
                for q in range(QB):
                    last = dve.bn_stats(stats[:, q, :], src[:, b.mod(2), q, :])
                last.then_inc(stats_done, 1)
                wait(dve, stats_done, b.times(1, 1))

            def norm_mean_variance(stats, mv, mv_ready, b):
                for q in range(QB):
                    last = dve.bn_aggr(mv[:, b.mod(2), q, :], stats[:, q, :])
                last.then_inc(mv_ready, 1)

            def stats_in(t):
                b = t + 2
                wait(dve, x_loaded[b.mod(2)], b.turn(2, 16, 16))
                wait(dve, xn1_ready, b.times(1, -1))
                wait(dve, mv1_ready, b.times(1))
                norm_stats(x_in, stats1, stats1_done, b)

            def qk_mid(t):
                b = t + 1
                wait(dve, qk_hi_ready, b.times(1, 1))
                wait(dve, qk_lo_ready, b.times(1))
                dve.tensor_tensor(qk_rest[:, :, :], ps_qk[:, :, :], qk_parts[:, b.mod(2), 0, :, :],
                                  ALU.subtract).then_inc(qk_rest_ready, 1)
                wait(dve, qk_rest_ready, b.times(1, 1))
                dve.tensor_copy(qk_parts[:, b.mod(2), 1, :, :], qk_rest[:, :, :]).then_inc(qk_mid_ready, 1)

            def row_max(b, h):
                wait(dve, scores_done, b.times(H, h + 1))
                dve.tensor_reduce(neg_max[:, b.mod(2), :, h], ps_s[h % 2][:, :, :], AX.X, ALU.max,
                                  negate=True).then_inc(max_done, 1)

            def split_max(t):
                b = t - 1
                wait(dve, max_done, b.times(H, H))
                wait(dve, mT_done, b.times(1))
                nm = neg_max[:, b.mod(2), :, :]
                dve.tensor_copy(m_parts[:, :, 0, :], nm).then_inc(m_hi_ready, 1)
                wait(dve, m_hi_ready, b.times(1, 1))
                dve.tensor_tensor(m_rest[:, :, :], nm, m_parts[:, :, 0, :], ALU.subtract).then_inc(m_rest_ready, 1)
                wait(dve, m_rest_ready, b.times(1, 1))
                dve.tensor_copy(m_parts[:, :, 1, :], m_rest[:, :, :]).then_inc(m_mid_ready, 1)
                wait(dve, m_mid_ready, b.times(1, 1))
                dve.tensor_tensor(m_parts[:, :, 2, :], m_rest[:, :, :], m_parts[:, :, 1, :],
                                  ALU.subtract).then_inc(m_lo_ready, 1)

            def mT_copy(t):
                b = t - 1
                wait(dve, mT_done, b.times(1, 1))
                wait(dve, m_stacked[(b - 1).mod(2)], (b - 1).turn(2, 16, 16))
                dve.tensor_copy(mT[:, :], ps_shared_bf[0:PARTS * H, 0:S]).then_inc(shared_free, 1)

            def normalise(b, q):
                wait(dve, ot_done, b.times(QB, q + 1))
                heads = ps_ot[:, :, :].rearrange("p g (j c) -> p (g j) c", c=VW)
                dve.reciprocal(rden[:, :], heads[:, :, DH]).then_inc(rden_ready, 1)
                wait(dve, rden_ready, b.times(QB, q + 1))
                wait(dve, concT_done, b.times(1))
                dve.tensor_tensor(conc[:, q, :, :], heads[:, :, 0:DH],
                                  rden[:, :].unsqueeze(2).broadcast_to([P, H, DH]),
                                  ALU.mult).then_inc(conc_ready, 1)

            def residual(t):
                b = t - 3
                wait(dve, wo_done, b.times(1, 1))
                wait(dve, xb_ready, b.times(1, 1))
                wait(dve, xn2_ready, b.times(1, -1))
                dve.tensor_tensor(x1[:, b.mod(2), :, :], ps_shared[:, 0:QB * D].rearrange("p (q d) -> p q d", q=QB),
                                  xb[:, :, :], ALU.add).then_inc(shared_free, 1)
                wait(dve, shared_free, shared_after(t, "wo"))
                dve.tensor_copy(x1_all[:, bass.ds(b.times(QB), QB), :], x1[:, b.mod(2), :, :]).then_inc(x1_kept, 1)
                wait(dve, mv2_ready, b.times(1))
                norm_stats(x1, stats2, stats2_done, b)

            def step(t):
                a, l, m, e = t + 1, t + 2, t - 1, t - 3
                for h in range(H):
                    if h == 0 and m.on:
                        split_max(t)
                    if h == 4 and a.on:
                        qk_mid(t)
                    if h == 5 and e.on:
                        normalise(e, 0)
                    if h == 7 and m.on:
                        mT_copy(t)
                    if h == 9 and e.on:
                        normalise(e, 1)
                    if h == 11 and l.on:
                        stats_in(t)
                    if h == 12 and l.on:
                        norm_mean_variance(stats1, mv1, mv1_ready, l)
                    if h == 13 and e.on:
                        residual(t)
                    if h == 14 and e.on:
                        norm_mean_variance(stats2, mv2, mv2_ready, e)
                    if t.on:
                        row_max(t, h)

            steps(dve, step)


def moe(nc, router_w, w_fc, w_proj, shared_fc, shared_proj, x1_all, xn2T_all, out):
    D, NT = x1_all.shape[0], x1_all.shape[1]
    E, _, F = w_fc.shape
    FC = F // P
    C = 512
    Q = C // P
    CHUNKS = NT // Q
    NE = E + 1

    with ExitStack() as ctx:
        def sb(name, shape, dt=F32):
            return ctx.enter_context(nc.sbuf_tensor(name, shape, dt))

        def ps(name, shape):
            return ctx.enter_context(nc.psum_tensor(name, shape, F32))

        def sem(name):
            return ctx.enter_context(nc.semaphore(name))

        rw_sb = sb("rw_sb", [D, E])
        fc_sb = sb("fc_sb", [D, NE, F])
        proj_sb = sb("proj_sb", [P, NE, FC, D])
        probs = sb("r_probs", [P, NT, E])
        top = sb("r_top", [P, NT, 1])
        total = sb("r_total", [P, NT, 1])
        above = sb("r_above", [P, NT, E])
        rank = sb("r_rank", [P, NT, E])
        combine = sb("r_combine", [P, NT, NE])
        comb_now = sb("comb_now", [P, 2, Q, NE])
        relu = sb("relu", [P, 2, C])
        hid = sb("hid", [P, 2, FC, C])
        acc = sb("acc", [P, 2, Q, D])
        ps_r = ps("ps_r", [P, NT, E])
        ps_h = [ps(f"ps_h{n}", [P, C]) for n in range(3)]
        ps_y = [ps(f"ps_y{n}", [P, Q, D]) for n in range(2)]

        w_loaded = sem("w_loaded")
        logits_done = sem("logits_done")
        chain = sem("r_chain")
        exp_r = sem("exp_r")
        h_done = sem("h_done")
        relu_done = sem("relu_done")
        hid_done = sem("hid_done")
        y_done = sem("y_done")
        acc_done = sem("acc_done")
        comb_done = sem("comb_done")
        stored = [sem(f"stored{n}") for n in range(2)]
        out_v = out.rearrange("b s d -> (b s) d")
        block = ctx.enter_context(nc.Block())
        U2 = 2

        @block.sync
        def _(sp):
            sp.dma_start(rw_sb[:, :], router_w).then_inc(w_loaded, 16)
            sp.dma_start(fc_sb[:, 0:E, :], w_fc.rearrange("e d f -> d e f")).then_inc(w_loaded, 16)
            sp.dma_start(fc_sb[:, E, :], shared_fc).then_inc(w_loaded, 16)
            for e in range(E):
                sp.dma_start(proj_sb[:, e, :, :], w_proj[e].rearrange("(c p) d -> p c d", p=P)).then_inc(w_loaded, 16)
            sp.dma_start(proj_sb[:, E, :, :], shared_proj.rearrange("(c p) d -> p c d", p=P)).then_inc(w_loaded, 16)
            with sp.Fori(0, CHUNKS // U2) as i:
                for n in range(U2):
                    sp.wait_ge(acc_done, i * (U2 * NE) + NE * (n + 1))
                    sp.dma_start(out_v[bass.ds(i * (U2 * C) + n * C, C), :].rearrange("(q p) d -> p q d", p=P),
                                 acc[:, n, :, :]).then_inc(stored[n], 16)
            for n in range(U2):
                sp.wait_ge(stored[n], 16 * (CHUNKS // U2))

        @block.tensor
        def _(pe):
            pe.wait_ge(w_loaded, 16 * (E + 4))
            for t in range(NT):
                last = pe.matmul(ps_r[:, t, :], xn2T_all[:, t * P:(t + 1) * P], rw_sb[:, :], start=True, stop=True,
                                 skip_group_check=True)
            last.then_inc(logits_done, 1)
            with pe.Fori(0, CHUNKS // U2) as i:
                for n in range(U2):
                    for e in range(NE + 1):
                        if e < NE:
                            for f in range(FC):
                                u = (n * NE + e) * FC + f
                                if u >= 2:
                                    pe.wait_ge(relu_done, i * (U2 * NE * FC) + u - 1)
                                pe.matmul(ps_h[u % 2][:, :], fc_sb[:, e, f * P:(f + 1) * P],
                                          xn2T_all[:, bass.ds(i * (U2 * C) + n * C, C)],
                                          start=True, stop=True).then_inc(h_done, 1)
                        if e > 0:
                            k = n * NE + e - 1
                            pe.wait_ge(hid_done, i * (U2 * NE * FC) + (k + 1) * FC)
                            if k >= 2:
                                pe.wait_ge(acc_done, i * (U2 * NE) + k - 1)
                            for q in range(Q):
                                for f in range(FC):
                                    last = pe.matmul(ps_y[k % 2][:, q, :], hid[:, k % 2, f, q * P:(q + 1) * P],
                                                     proj_sb[:, e - 1, f, :], start=f == 0, stop=f == FC - 1,
                                                     skip_group_check=True)
                            last.then_inc(y_done, 1)
                pe.wait_ge(acc_done, i * (U2 * NE) + U2 * NE)

        @block.scalar
        def _(act):
            act.wait_ge(chain, 1)
            act.activation(probs[:, :, :], probs[:, :, :], ACT.Exp).then_inc(exp_r, 1)
            with act.Fori(0, CHUNKS // U2) as i:
                for u in range(U2 * NE * FC):
                    act.wait_ge(h_done, i * (U2 * NE * FC) + (u + 1))
                    if u >= 2:
                        act.wait_ge(hid_done, i * (U2 * NE * FC) + u - 1)
                    act.activation(relu[:, u % 2, :], ps_h[u % 2][:, :], ACT.Relu).then_inc(relu_done, 1)

        @block.vector
        def _(dve):
            count = [0]

            def link(ins):
                ins.then_inc(chain, 1)
                count[0] += 1
                dve.wait_ge(chain, count[0])

            def over(a, n=E):
                return a.broadcast_to([P, NT, n])

            dve.wait_ge(logits_done, 1)
            dve.tensor_reduce(top[:, :, 0], ps_r[:, :, :], AX.X, ALU.max).then_inc(exp_r, 1)
            dve.wait_ge(exp_r, 1)
            link(dve.tensor_tensor(probs[:, :, :], ps_r[:, :, :], over(top[:, :, :]), ALU.subtract))
            dve.wait_ge(exp_r, 2)
            link(dve.tensor_reduce(total[:, :, 0], probs[:, :, :], AX.X, ALU.add))
            link(dve.reciprocal(total[:, :, 0], total[:, :, 0]))
            link(dve.tensor_tensor(probs[:, :, :], probs[:, :, :], over(total[:, :, :]), ALU.mult))
            link(dve.memset(rank[:, :, :], 0.0))
            for e in range(E):
                one = probs[:, :, e:e + 1]
                if e > 0:
                    link(dve.tensor_tensor(above[:, :, 0:e], over(one, e), probs[:, :, 0:e], ALU.is_gt))
                if e < E - 1:
                    link(dve.tensor_tensor(above[:, :, e + 1:E], over(one, E - 1 - e), probs[:, :, e + 1:E], ALU.is_ge))
                link(dve.memset(above[:, :, e:e + 1], 0.0))
                link(dve.tensor_tensor(rank[:, :, :], rank[:, :, :], above[:, :, :], ALU.add))
            link(dve.tensor_scalar(rank[:, :, :], rank[:, :, :], 2.0, None, ALU.is_lt))
            link(dve.tensor_tensor(probs[:, :, :], probs[:, :, :], rank[:, :, :], ALU.mult))
            link(dve.tensor_reduce(total[:, :, 0], probs[:, :, :], AX.X, ALU.add))
            link(dve.tensor_scalar(total[:, :, 0], total[:, :, 0], 1e-9, None, ALU.max))
            link(dve.reciprocal(total[:, :, 0], total[:, :, 0]))
            link(dve.tensor_tensor(combine[:, :, 0:E], probs[:, :, :], over(total[:, :, :]), ALU.mult))
            link(dve.memset(combine[:, :, E:NE], 1.0))
            with dve.Fori(0, CHUNKS // U2) as i:
                for n in range(U2):
                    for e in range(NE + 1):
                        if e == 0:
                            dve.tensor_copy(comb_now[:, n, :, :],
                                            combine[:, bass.ds(i * (U2 * Q) + n * Q, Q), :]).then_inc(comb_done, 1)
                        for f in range(FC):
                            if e < NE:
                                u = (n * NE + e) * FC + f
                                dve.wait_ge(relu_done, i * (U2 * NE * FC) + (u + 1))
                                if n * NE + e >= 2 and f == 0:
                                    dve.wait_ge(y_done, i * (U2 * NE) + n * NE + e - 1)
                                dve.tensor_tensor(hid[:, (n * NE + e) % 2, f, :], relu[:, u % 2, :], relu[:, u % 2, :],
                                                  ALU.mult).then_inc(hid_done, 1)
                        if e > 0:
                            k = n * NE + e - 1
                            dve.wait_ge(y_done, i * (U2 * NE) + (k + 1))
                            if e == 1:
                                dve.wait_ge(comb_done, i * U2 + (n + 1))
                            else:
                                dve.wait_ge(acc_done, i * (U2 * NE) + k)
                            for q in range(Q):
                                base = acc[:, n, q, :] if e > 1 else x1_all[:, bass.ds(i * (U2 * Q) + n * Q + q, 1), :
                                                                            ].rearrange("p a d -> p (a d)")
                                last = dve.scalar_tensor_tensor(acc[:, n, q, :], ps_y[k % 2][:, q, :],
                                                                comb_now[:, n, q, e - 1:e], base, ALU.mult, ALU.add)
                            last.then_inc(acc_done, 1)
                    dve.wait_ge(stored[n], i * 16 + 16)


_INS = ["x", "wq", "wk", "wv", "wo", "bo", "router_w", "w_fc", "w_proj", "shared_fc", "shared_proj"]


def build(nc, x, wq, wk, wv, wo, bo, router_w, w_fc, w_proj, shared_fc, shared_proj, out):
    B, S, D = x.shape
    with ExitStack() as ctx:
        x1_all = ctx.enter_context(nc.sbuf_tensor("x1_all", [P, B * S // P, D], F32))
        xn2T_all = ctx.enter_context(nc.sbuf_tensor("xn2T_all", [D, B * S], F32))
        attention(nc, x, wq, wk, wv, wo, bo, x1_all, xn2T_all)
        moe(nc, router_w, w_fc, w_proj, shared_fc, shared_proj, x1_all, xn2T_all, out)


def kernel(**inputs):
    import numpy as _np
    import concourse.bacc as _bacc
    from concourse import mybir as _mybir
    from concourse.bass_utils import run_bass_kernel_spmd as _run

    a = {k: _np.asarray(v) for k, v in inputs.items()}
    d, heads = a["L0_attn_wq"].shape[0], 16

    def by_depth(w):
        return w.reshape(d, heads, -1).transpose(0, 2, 1).reshape(w.shape)

    laid = {
        "x": a["L0_attn_x"],
        "wq": by_depth(a["L0_attn_wq"]),
        "wk": by_depth(a["L0_attn_wk"]),
        "wv": a["L0_attn_wv"],
        "wo": a["L0_attn_wo"],
        "bo": a["L0_attn_bo"],
        "router_w": a["L0_ffn_router_w"].T,
        "w_fc": a["L0_ffn_w_fc"].transpose(0, 2, 1),
        "w_proj": a["L0_ffn_w_proj"].transpose(0, 2, 1),
        "shared_fc": a["L0_ffn_shared_fc"].T,
        "shared_proj": a["L0_ffn_shared_proj"].T,
    }
    nc = _bacc.Bacc("TRN2", target_bir_lowering=False, num_devices=1)
    arrays, args = {}, []
    for name in _INS:
        v = _np.ascontiguousarray(laid[name])
        arrays[f"in_{name}"] = v
        args.append(nc.dram_tensor(f"in_{name}", v.shape, _mybir.dt.from_np(v.dtype), kind="ExternalInput").ap())
    out = nc.dram_tensor("out", a["L0_attn_x"].shape, _mybir.dt.float32, kind="ExternalOutput").ap()
    build(nc, *args, out)
    r = _run(nc, [arrays], core_ids=[0])
    return r.results[0]["out"]
```

```python
import concourse.bass as bass
from concourse import mybir
from contextlib import ExitStack

F32 = mybir.dt.float32
BF16 = mybir.dt.bfloat16
I32 = mybir.dt.int32
ALU = mybir.AluOpType
ACT = mybir.ActivationFunctionType
AX = mybir.AxisListType

P = 128
TILE = 512
EPS = 1e-5
U = 4


class Batch:

    def __init__(self, i, c, total, unroll=U):
        self.i, self.c, self.total, self.unroll = i, c, total, unroll

    def __add__(self, n):
        return Batch(self.i, self.c + n, self.total, self.unroll)

    def __sub__(self, n):
        return self + (-n)

    @property
    def on(self):
        return self.i is not None or 0 <= self.c < self.total

    def mod(self, m):
        return self.c % m

    def times(self, k, n=0):
        return k * self.c + n if self.i is None else self.i * (k * self.unroll) + (k * self.c + n)

    def turn(self, m, k, n=0):
        return k * (self.c // m) + n if self.i is None else self.i * (k * (self.unroll // m)) + (k * (self.c // m) + n)


def wait(eng, sem, value):
    if isinstance(value, int) and value <= 0:
        return
    eng.wait_ge(sem, value)


SHARED_USES = [("xnT", 2), ("v", 1), ("mT", -1), ("xn2T", -4), ("concT", -3), ("wo", -3)]


def shared_use(t, name):
    at = [n for n, _ in SHARED_USES].index(name)

    def before(step, upto):
        return sum(0 <= s + d < t.total for s in range(-U, step) for _, d in SHARED_USES) + sum(
            0 <= step + d < t.total for _, d in SHARED_USES[:upto])

    if t.i is None:
        return before(t.c, at)
    return t.i * (U * len(SHARED_USES)) + (before(U, 0) + (t.c - U) * len(SHARED_USES) + at)


def shared_after(t, name):
    return shared_use(t, name) + 1


def attention(nc, x, wq, wk, wv, wo, bo, xn2T_all, rows, slot_rows, TILES, out):
    B, S, D = x.shape
    H = 16
    DH = D // H
    QB = S // P
    G = H // 4
    VW = 32
    PARTS = 3
    KR = PARTS * PARTS * DH
    KS = 96
    KM = KS + PARTS
    SCALE = float(DH) ** -0.5
    NT = B * QB
    FIRST, LOOPED = -3, U
    TURNS = (B - 4 - U) // U
    LAST = B + 4
    STORED = 16 * (1 + PARTS)
    STACKED = 16 * (PARTS + 1)

    with ExitStack() as ctx:
        def sb(name, shape, dt=F32):
            return ctx.enter_context(nc.sbuf_tensor(name, shape, dt))

        def ps(name, shape):
            return ctx.enter_context(nc.psum_tensor(name, shape, F32))

        def sem(name):
            return ctx.enter_context(nc.semaphore(name))

        ident = sb("ident", [P, P])
        minus_half = sb("minus_half", [P, QB])
        eps_sb = sb("eps_sb", [P, QB])
        wq_sb, wk_sb, wv_sb, wo_sb = (sb(n, [D, D]) for n in ("wq_sb", "wk_sb", "wv_sb", "wo_sb"))
        bo_sb = sb("bo_sb", [P, D])
        x_in = sb("x_in", [P, 2, QB, D])
        stats1 = sb("stats1", [P, QB, 6])
        mv1 = sb("mv1", [P, 2, QB, 2])
        centred1 = sb("centred1", [P, QB, D])
        rstd1 = sb("rstd1", [P, QB])
        xn1 = sb("xn1", [P, 2, QB, D])
        xnT = sb("xnT", [D, 2, S])
        qk_parts = sb("qk_parts", [P, 2, PARTS, 2, S], BF16)
        qk_rest = sb("qk_rest", [P, 2, S])
        q_stack = sb("q_stack", [KM, U, H, S], BF16)
        k_stack = sb("k_stack", [KM, U, H, S], BF16)
        filler = sb("filler", [P, 2, P], BF16)
        no_rows = sb("no_rows", [P, TILE // P, D + 2])
        ident_bf = sb("ident_bf", [P, P], BF16)
        v_aug = sb("v_aug", [P, U, QB, H, VW])
        neg_max = sb("neg_max", [P, 2, QB, H])
        m_parts = sb("m_parts", [P, QB, P // H, H], BF16)
        m_rest = sb("m_rest", [P, QB, H])
        mT = sb("mT", [PARTS * H, S], BF16)
        probs = sb("probs", [P, 8, QB, S])
        o_sb = sb("o_sb", [P, 2, G, S])
        rden = sb("rden", [P, H])
        conc = sb("conc", [P, QB, H, DH])
        concT = sb("concT", [D, S])
        x_res = sb("x_res", [P, 2, QB, D])
        xb = sb("xb", [P, QB, D])
        x1 = sb("x1", [P, 2, QB, D])
        stats2 = sb("stats2", [P, QB, 6])
        mv2 = sb("mv2", [P, 2, QB, 2])
        centred2 = sb("centred2", [P, QB, D])
        rstd2 = sb("rstd2", [P, QB])
        xn2 = sb("xn2", [P, QB, D])

        q_dram = nc.dram_tensor("q_parts", (2, PARTS, DH, H, S), BF16, kind="Internal").ap()
        k_dram = nc.dram_tensor("k_parts", (2, PARTS, PARTS, DH, H, S), BF16, kind="Internal").ap()

        ps_s = [ps(f"ps_s{n}", [P, QB, S]) for n in range(3)]
        ps_st = [ps(f"ps_st{n}", [P, QB, S]) for n in range(2)]
        ps_o = ps("ps_o", [P, 512])
        ps_turn = ps("ps_turn", [P, 512])
        ps_ot = ps_turn[:, :].rearrange("p (g t) -> p g t", g=G)
        ps_qk = ps_turn[:, :].rearrange("p (i t) -> p i t", i=2)
        ps_shared = ps("ps_shared", [P, 512])
        ps_shared_bf = ps_shared[:, :].bitcast(BF16)

        consts_loaded = sem("consts_loaded")
        consts_ready = sem("consts_ready")
        half_ready = sem("half_ready")
        vpad_ready = sem("vpad_ready")
        rows_filled = sem("rows_filled")
        x_loaded = [sem(f"x_loaded{n}") for n in range(2)]
        stats1_done = sem("stats1_done")
        mv1_ready = sem("mv1_ready")
        rstd1_steps = sem("rstd1_steps")
        xn1_ready = sem("xn1_ready")
        xnT_done = sem("xnT_done")
        qk_done = sem("qk_done")
        qk_hi_ready = sem("qk_hi_ready")
        qk_rest_ready = sem("qk_rest_ready")
        qk_mid_ready = sem("qk_mid_ready")
        qk_lo_ready = sem("qk_lo_ready")
        parts_stored = [sem(f"parts_stored{n}") for n in range(2)]
        v_done = sem("v_done")
        stacked = [sem(f"stacked{n}") for n in range(2)]
        scores_done = sem("scores_done")
        max_done = sem("max_done")
        m_hi_ready = sem("m_hi_ready")
        m_rest_ready = sem("m_rest_ready")
        m_mid_ready = sem("m_mid_ready")
        m_lo_ready = sem("m_lo_ready")
        mT_done = sem("mT_done")
        m_stacked = [sem(f"m_stacked{n}") for n in range(2)]
        scoresT_done = sem("scoresT_done")
        exp_done = sem("exp_done")
        pv_done = sem("pv_done")
        o_ready = sem("o_ready")
        ot_done = sem("ot_done")
        rden_ready = sem("rden_ready")
        conc_ready = sem("conc_ready")
        concT_done = sem("concT_done")
        wo_done = sem("wo_done")
        xres_loaded = [sem(f"xres_loaded{n}") for n in range(2)]
        xb_ready = sem("xb_ready")
        x1_stored = [sem(f"x1_stored{n}") for n in range(2)]
        rows_kept = sem("rows_kept")
        no_rows_ready = sem("no_rows_ready")
        slots_filled = sem("slots_filled")
        stats2_done = sem("stats2_done")
        mv2_ready = sem("mv2_ready")
        rstd2_steps = sem("rstd2_steps")
        xn2_ready = sem("xn2_ready")
        xn2T_done = sem("xn2T_done")
        shared_free = sem("shared_free")

        S_BANK = [h % 3 for h in range(H - 1)] + [1]
        S_AGO = [next(n for n in range(1, H) if S_BANK[h - n] == S_BANK[h]) for h in range(H)]

        x_rows = x.rearrange("b s d -> (b s) d")

        out_rows = out

        def x_batch(row):
            rows = x_rows[bass.ds(row, S), :]
            return rows.rearrange("(q p) d -> p q d", p=P)

        def steps(eng, step):
            for c in range(FIRST, LOOPED):
                step(Batch(None, c, B))
            with eng.Fori(0, TURNS) as i:
                for c in range(LOOPED, LOOPED + U):
                    step(Batch(i, c, B))
            for c in range(LOOPED + U * TURNS, LAST + 1):
                step(Batch(None, c, B))

        block = ctx.enter_context(nc.Block())

        @block.sync
        def _(sp):
            for w, src in ((wq_sb, wq), (wk_sb, wk), (wv_sb, wv), (wo_sb, wo)):
                sp.dma_start(w[:, :], src).then_inc(consts_loaded, 16)
            sp.dma_start(bo_sb[:, :], bo.rearrange("(a n) -> a n", a=1).broadcast_to([P, D])).then_inc(consts_loaded, 16)

            sp.wait_ge(consts_ready, 5)
            for n in range(U):
                for stack in (q_stack, k_stack):
                    sp.dma_start(stack[KR:KS, n, :, :].rearrange("p h t -> p (h t)"),
                                 filler[:, 0:1, :].broadcast_to([P, (KS - KR) * H * S // P // P, P])
                                 ).then_inc(rows_filled, 16)
                sp.dma_start(k_stack[KS:KM, n, :, :].rearrange("p h t -> p (h t)"),
                             filler[0:96, 1:2, :].broadcast_to([96, PARTS * H * S // P // 96, P])
                             ).then_inc(rows_filled, 16)

            def fill_slots(tile):
                sp.dma_start(slot_rows[bass.ds(tile, TILE), :].rearrange("(q p) d -> p q d", p=P),
                             no_rows[:, :, :]).then_inc(slots_filled, 16)

            sp.wait_ge(no_rows_ready, 2)
            sp.dma_start(out[B * S:B * S + TILE, :].rearrange("(q p) d -> p q d", p=P),
                         no_rows[:, :, 0:D]).then_inc(slots_filled, 16)
            for n in range(LAST + 1 - FIRST, TILES):
                fill_slots(n * TILE)

            def step(t):
                b = t + 1
                if b.on:
                    wait(sp, scoresT_done, b.times(H, -(U - 1) * H))
                if t.i is not None or t.c - FIRST < TILES:
                    fill_slots(t.times(TILE, -FIRST * TILE))
                if b.on:
                    wait(sp, parts_stored[b.mod(2)], b.turn(2, STORED, STORED))
                    for j in range(PARTS):
                        at = j * PARTS * DH
                        sp.dma_start(q_stack[at:at + PARTS * DH, b.mod(U), :, :],
                                     q_dram[b.mod(2)].rearrange("i d h t -> (i d) h t")
                                     ).then_inc(stacked[b.mod(2)], 16)
                    sp.dma_start(k_stack[0:KR, b.mod(U), :, :],
                                 k_dram[b.mod(2)].rearrange("j i d h t -> (j i d) h t")
                                 ).then_inc(stacked[b.mod(2)], 16)
                b = t + 4
                if t.c == FIRST and t.i is None:
                    sp.dma_start(x_in[:, 0, :, :], x_batch(0)).then_inc(x_loaded[0], 16)
                if b.on:
                    wait(sp, xn1_ready, b.times(1, -1))
                    sp.dma_start(x_in[:, b.mod(2), :, :], x_batch(b.times(S))).then_inc(x_loaded[b.mod(2)], 16)
                b = t - 2
                if b.on:
                    wait(sp, xb_ready, b.times(1, -1))
                    sp.dma_start(x_res[:, b.mod(2), :, :], x_batch(b.times(S))).then_inc(xres_loaded[b.mod(2)], 16)
                b = t - 4
                if b.on:
                    wait(sp, stats2_done, b.times(1, 1))
                    sp.dma_start(out_rows[bass.ds(b.times(S), S), :].rearrange("(q p) d -> p q d", p=P),
                                 x1[:, b.mod(2), :, :]).then_inc(x1_stored[b.mod(2)], 16)
                b = t - 1
                if b.on:
                    wait(sp, shared_free, shared_after(t, "mT"))
                    sp.dma_start(q_stack[KS:KM, b.mod(U), :, :], mT[:, :]).then_inc(m_stacked[b.mod(2)], 16)
                b = t + 2
                if b.on:
                    wait(sp, qk_lo_ready, b.times(1, 1))
                    part = qk_parts[:, b.mod(2), :, :, :]
                    sp.dma_start(q_dram[b.mod(2)].rearrange("i d h t -> (d h) i t"),
                                 part[:, :, 0, :]).then_inc(parts_stored[b.mod(2)], 16)
                    for i in range(PARTS):
                        sp.dma_start(k_dram[b.mod(2), :, i].rearrange("j d h t -> (d h) j t"),
                                     part[:, :, 1, :]).then_inc(parts_stored[b.mod(2)], 16)

            steps(sp, step)
            sp.wait_ge(slots_filled, 16 * (1 + TILES))
            for n in range(2):
                sp.wait_ge(x1_stored[n], 16 * (B // 2))
        @block.gpsimd
        def _(pool):
            pool.memset(ident[:, :], 0.0).then_inc(consts_ready, 1)
            pool.wait_ge(consts_ready, 1)
            pool.affine_select(out=ident[:, :], in_=ident[:, :], compare_op=ALU.not_equal, fill=1.0, base=0,
                               pattern=[[-1, P]], channel_multiplier=1).then_inc(consts_ready, 1)
            pool.wait_ge(consts_ready, 2)
            pool.memset(filler[:, 0, :], 0.0).then_inc(consts_ready, 1)
            pool.memset(filler[:, 1, :], 1.0).then_inc(consts_ready, 1)
            pool.tensor_copy(ident_bf[:, :], ident[:, :]).then_inc(consts_ready, 1)
            pool.memset(no_rows[:, :, :], 0.0).then_inc(no_rows_ready, 1)
            pool.wait_ge(no_rows_ready, 1)
            pool.iota(no_rows[:, :, D + 1].bitcast(I32), pattern=[[P, TILE // P]], base=B * S,
                      channel_multiplier=1).then_inc(no_rows_ready, 1)
            pool.memset(minus_half[:, :], -0.5).then_inc(half_ready, 1)
            pool.memset(eps_sb[:, :], EPS).then_inc(half_ready, 1)
            pool.wait_ge(half_ready, 2)
            pool.wait_ge(consts_loaded, 16 * 5)

            def normalise(mv, centred, rs, out_, src, chain, b):
                pool.tensor_tensor(rs[:, :], mv[:, b.mod(2), :, 1], eps_sb[:, :], ALU.add).then_inc(chain, 1)
                pool.tensor_tensor(centred[:, :, :], src,
                                   mv[:, b.mod(2), :, 0:1].broadcast_to([P, QB, D]), ALU.subtract).then_inc(chain, 1)
                wait(pool, chain, b.times(3, 1))
                pool.tensor_tensor(rs[:, :], rs[:, :], minus_half[:, :], ALU.pow).then_inc(chain, 1)
                wait(pool, chain, b.times(3, 3))
                return pool.tensor_tensor(out_, centred[:, :, :], rs[:, :].unsqueeze(2).broadcast_to([P, QB, D]),
                                          ALU.mult)

            def step(t):
                b = t - 3
                if b.on:
                    wait(pool, xres_loaded[b.mod(2)], b.turn(2, 16, 16))
                    wait(pool, stats2_done, b.times(1))
                    for q in range(QB):
                        last = pool.tensor_tensor(xb[:, q, :], x_res[:, b.mod(2), q, :], bo_sb[:, :], ALU.add)
                    last.then_inc(xb_ready, 1)
                b = t + 3
                if b.on:
                    wait(pool, mv1_ready, b.times(1, 1))
                    wait(pool, xn1_ready, b.times(1))
                    wait(pool, xnT_done, b.times(1, -1))
                    normalise(mv1, centred1, rstd1, xn1[:, b.mod(2), :, :], x_in[:, b.mod(2), :, :],
                              rstd1_steps, b).then_inc(xn1_ready, 1)
                b = t + 2
                if b.on:
                    wait(pool, qk_mid_ready, b.times(1, 1))
                    pool.tensor_tensor(qk_parts[:, b.mod(2), 2, :, :], qk_rest[:, :, :],
                                       qk_parts[:, b.mod(2), 1, :, :], ALU.subtract).then_inc(qk_lo_ready, 1)
                b = t - 3
                if b.on:
                    wait(pool, mv2_ready, b.times(1, 1))
                    wait(pool, xn2_ready, b.times(1))
                    wait(pool, rows_kept, b.times(1))
                    normalise(mv2, centred2, rstd2, xn2[:, :, :], x1[:, b.mod(2), :, :],
                              rstd2_steps, b).then_inc(xn2_ready, 1)

            steps(pool, step)

        @block.tensor
        def _(pe):
            pe.wait_ge(consts_ready, 5)
            pe.wait_ge(consts_loaded, 16 * 5)
            pe.wait_ge(vpad_ready, 2)
            pe.wait_ge(rows_filled, 16 * 3 * U)

            def xnT_use(t):
                b = t + 2
                wait(pe, shared_free, shared_use(t, "xnT"))
                wait(pe, xn1_ready, b.times(1, 1))
                for q in range(QB):
                    last = pe.transpose(ps_shared[:, q * P:(q + 1) * P], xn1[:, b.mod(2), q, :], ident[:, :])
                last.then_inc(xnT_done, 1)

            def project_qk(t):
                b = t + 2
                wait(pe, shared_free, shared_after(t, "xnT"))
                wait(pe, conc_ready, b.times(QB, -4 * QB))
                pe.matmul(ps_qk[:, 0, :], wq_sb[:, :], xnT[:, b.mod(2), :], start=True, stop=True)
                pe.matmul(ps_qk[:, 1, :], wk_sb[:, :], xnT[:, b.mod(2), :], start=True, stop=True,
                          skip_group_check=True).then_inc(qk_done, 1)

            def project_v(t):
                b = t + 1
                wait(pe, shared_free, shared_use(t, "v"))
                for q in range(QB):
                    last = pe.matmul(ps_shared[:, q * D:(q + 1) * D], xnT[:, b.mod(2), q * P:(q + 1) * P], wv_sb[:, :],
                                     start=True, stop=True, skip_group_check=True)
                last.then_inc(v_done, 1)

            def scores(b, h):
                if h == 0:
                    wait(pe, stacked[b.mod(2)], b.turn(2, STACKED, STACKED))
                wait(pe, max_done, b.times(H, h + 1 - S_AGO[h]))
                for q in range(QB):
                    last = pe.matmul(ps_s[S_BANK[h]][:, q, :], q_stack[0:KS, b.mod(U), h, q * P:(q + 1) * P],
                                     k_stack[0:KS, b.mod(U), h, :], start=True, stop=True, skip_group_check=True)
                last.then_inc(scores_done, 1)

            def maxT(t):
                b = t - 1
                wait(pe, shared_free, shared_use(t, "mT"))
                wait(pe, m_lo_ready, b.times(1, 1))
                for q in range(QB):
                    last = pe.transpose(ps_shared_bf[:, q * P:(q + 1) * P],
                                        m_parts[:, q, :, :].rearrange("p i h -> p (i h)"), ident_bf[:, :])
                last.then_inc(mT_done, 1)

            def scoresT(b, h):
                if h == 0:
                    wait(pe, m_stacked[b.mod(2)], b.turn(2, 16, 16))
                wait(pe, exp_done, b.times(H, h - 1))
                for k in range(QB):
                    last = pe.matmul(ps_st[h % 2][:, k, :], k_stack[0:KM, b.mod(U), h, k * P:(k + 1) * P],
                                     q_stack[0:KM, b.mod(U), h, :], start=True, stop=True, skip_group_check=True)
                last.then_inc(scoresT_done, 1)

            def pv(b, g):
                wait(pe, exp_done, b.times(H, 4 * g + 4))
                wait(pe, o_ready, b.times(G, g))
                for k in range(QB):
                    for j in range(4):
                        h = 4 * g + j
                        last = pe.matmul(ps_o[32 * j:32 * j + VW, 0:S], v_aug[:, b.mod(U), k, h, :],
                                         probs[:, h % 8, k, :], start=k == 0, stop=k == QB - 1,
                                         skip_group_check=True)
                last.then_inc(pv_done, 1)

            def oT(b, q):
                wait(pe, o_ready, b.times(G, G))
                if q == 0:
                    wait(pe, qk_rest_ready, b.times(1, 5) if b.i is not None else min(b.c + 5, B))
                else:
                    wait(pe, conc_ready, b.times(QB, q))
                for g in range(G):
                    last = pe.transpose(ps_ot[:, g, :], o_sb[:, b.mod(2), g, q * P:(q + 1) * P], ident[:, :])
                last.then_inc(ot_done, 1)

            def xn2T_use(t):
                b = t - 4
                wait(pe, shared_free, shared_use(t, "xn2T"))
                wait(pe, xn2_ready, b.times(1, 1))
                for q in range(QB):
                    last = pe.transpose(ps_shared[:, q * P:(q + 1) * P], xn2[:, q, :], ident[:, :])
                last.then_inc(xn2T_done, 1)

            def concT_use(t):
                b = t - 3
                wait(pe, shared_free, shared_use(t, "concT"))
                wait(pe, conc_ready, b.times(QB, QB))
                for q in range(QB):
                    last = pe.transpose(ps_shared[:, q * P:(q + 1) * P],
                                        conc[:, q, :, :].rearrange("p h d -> p (h d)"), ident[:, :])
                last.then_inc(concT_done, 1)

            def project_o(t):
                wait(pe, shared_free, shared_after(t, "concT"))
                for q in range(QB):
                    last = pe.matmul(ps_shared[:, q * D:(q + 1) * D], concT[:, q * P:(q + 1) * P], wo_sb[:, :],
                                     start=True, stop=True, skip_group_check=True)
                last.then_inc(wo_done, 1)

            def step(t):
                l, a, m, c, e, f = t + 2, t + 1, t - 1, t - 2, t - 3, t - 4
                for h in range(H):
                    if h == 0 and l.on:
                        xnT_use(t)
                    if h == 3 and a.on:
                        project_v(t)
                    if h == 13 and l.on:
                        project_qk(t)
                    if h == 5 and m.on:
                        maxT(t)
                    if h == 8 and f.on:
                        xn2T_use(t)
                    if h == 12 and e.on:
                        concT_use(t)
                    if h == 14 and e.on:
                        project_o(t)
                    if t.on:
                        scores(t, h)
                    if c.on:
                        scoresT(c, h)
                    if h == 1 and e.on:
                        pv(e, G - 1)
                    if h in (5, 9, 13) and c.on:
                        pv(c, h // 4 - 1)
                    if h in (4, 8) and e.on:
                        oT(e, h // 8)

            steps(pe, step)

        @block.scalar
        def _(act):
            def xnT_copy(t):
                b = t + 2
                wait(act, xnT_done, b.times(1, 1))
                wait(act, v_done, b.times(1, -1))
                act.activation(xnT[:, b.mod(2), :], ps_shared[:, 0:S], ACT.Copy).then_inc(shared_free, 1)

            def q_hi(t):
                b = t + 2
                wait(act, qk_done, b.times(1, 1))
                wait(act, parts_stored[b.mod(2)], b.turn(2, STORED))
                act.activation(qk_parts[:, b.mod(2), 0, :, :], ps_qk[:, :, :], ACT.Copy).then_inc(qk_hi_ready, 1)

            def v_copy(t):
                b = t + 1
                wait(act, v_done, b.times(1, 1))
                wait(act, pv_done, b.times(G, -(U - 1) * G))
                act.activation(v_aug[:, b.mod(U), :, :, 0:DH],
                               ps_shared[:, 0:QB * D].rearrange("p (q h d) -> p q h d", q=QB, h=H),
                               ACT.Copy).then_inc(shared_free, 1)

            def exp(b, h):
                wait(act, scoresT_done, b.times(H, h + 1))
                if h % 4 == 0:
                    wait(act, pv_done, b.times(G, h // 4 - 1))
                act.activation(probs[:, h % 8, :, :], ps_st[h % 2][:, :, :], ACT.Exp,
                               scale=SCALE).then_inc(exp_done, 1)

            def o_copy(b, g):
                wait(act, pv_done, b.times(G, g + 1))
                if g == 0:
                    wait(act, ot_done, b.times(QB, -QB))
                act.activation(o_sb[:, b.mod(2), g, :], ps_o[:, 0:S], ACT.Copy).then_inc(o_ready, 1)

            def xn2T_copy(t):
                b = t - 4
                wait(act, xn2T_done, b.times(1, 1))
                act.activation(xn2T_all[:, bass.ds(b.times(S), S)], ps_shared[:, 0:S], ACT.Copy).then_inc(shared_free, 1)

            def rows_copy(t):
                b = t - 4
                wait(act, xn2_ready, b.times(1, 1))
                act.activation(rows[:, bass.ds(b.times(QB), QB), 0:D], xn2[:, :, :], ACT.Copy).then_inc(rows_kept, 1)

            def concT_copy(t):
                b = t - 3
                wait(act, concT_done, b.times(1, 1))
                act.activation(concT[:, :], ps_shared[:, 0:S], ACT.Copy).then_inc(shared_free, 1)

            def qk_mid(t):
                b = t + 2
                wait(act, qk_rest_ready, b.times(1, 1))
                act.activation(qk_parts[:, b.mod(2), 1, :, :], qk_rest[:, :, :], ACT.Copy).then_inc(qk_mid_ready, 1)

            def mT_copy(t):
                b = t - 1
                wait(act, mT_done, b.times(1, 1))
                wait(act, m_stacked[(b - 1).mod(2)], (b - 1).turn(2, 16, 16))
                act.activation(mT[:, :], ps_shared_bf[0:PARTS * H, 0:S], ACT.Copy).then_inc(shared_free, 1)

            def step(t):
                l, a, m, c, e, f = t + 2, t + 1, t - 1, t - 2, t - 3, t - 4
                for h in range(H):
                    if h == 0 and l.on:
                        xnT_copy(t)
                    if h == 3 and a.on:
                        v_copy(t)
                    if h == 2 and e.on:
                        o_copy(e, G - 1)
                    if h == 5 and m.on:
                        mT_copy(t)
                    if h in (6, 10, 14) and c.on:
                        o_copy(c, h // 4 - 1)
                    if h == 8 and f.on:
                        xn2T_copy(t)
                    if h == 12 and e.on:
                        concT_copy(t)
                    if c.on:
                        exp(c, h)
                    if h == 13 and l.on:
                        q_hi(t)
                    if h == 15 and l.on:
                        qk_mid(t)
                    if h == 9 and f.on:
                        rows_copy(t)

            steps(act, step)

        @block.vector
        def _(dve):
            dve.memset(m_parts[:, :, PARTS:P // H, :], 0.0)
            dve.memset(v_aug[:, :, :, :, DH:VW], 0.0).then_inc(vpad_ready, 1)
            dve.wait_ge(vpad_ready, 1)
            dve.memset(v_aug[:, :, :, :, DH:DH + 1], 1.0).then_inc(vpad_ready, 1)

            def norm_stats(src, stats, stats_done, b):
                for q in range(QB):
                    last = dve.bn_stats(stats[:, q, :], src[:, b.mod(2), q, :])
                last.then_inc(stats_done, 1)
                wait(dve, stats_done, b.times(1, 1))

            def norm_mean_variance(stats, mv, mv_ready, b):
                for q in range(QB):
                    last = dve.bn_aggr(mv[:, b.mod(2), q, :], stats[:, q, :])
                last.then_inc(mv_ready, 1)

            def stats_in(t):
                b = t + 3
                wait(dve, x_loaded[b.mod(2)], b.turn(2, 16, 16))
                wait(dve, xn1_ready, b.times(1, -1))
                wait(dve, mv1_ready, b.times(1))
                norm_stats(x_in, stats1, stats1_done, b)

            def qk_left(t):
                b = t + 2
                wait(dve, qk_hi_ready, b.times(1, 1))
                wait(dve, qk_lo_ready, b.times(1))
                dve.tensor_tensor(qk_rest[:, :, :], ps_qk[:, :, :], qk_parts[:, b.mod(2), 0, :, :],
                                  ALU.subtract).then_inc(qk_rest_ready, 1)

            def row_max(b, h):
                wait(dve, scores_done, b.times(H, h + 1))
                dve.tensor_reduce(neg_max[:, b.mod(2), :, h], ps_s[S_BANK[h]][:, :, :], AX.X, ALU.max,
                                  negate=True).then_inc(max_done, 1)

            def split_max(t, part):
                b = t - 1
                nm = neg_max[:, b.mod(2), :, :]
                if part == 0:
                    wait(dve, max_done, b.times(H, H))
                    wait(dve, mT_done, b.times(1))
                    dve.tensor_copy(m_parts[:, :, 0, :], nm).then_inc(m_hi_ready, 1)
                elif part == 1:
                    wait(dve, m_hi_ready, b.times(1, 1))
                    dve.tensor_tensor(m_rest[:, :, :], nm, m_parts[:, :, 0, :], ALU.subtract).then_inc(m_rest_ready, 1)
                elif part == 2:
                    wait(dve, m_rest_ready, b.times(1, 1))
                    dve.tensor_copy(m_parts[:, :, 1, :], m_rest[:, :, :]).then_inc(m_mid_ready, 1)
                else:
                    wait(dve, m_mid_ready, b.times(1, 1))
                    dve.tensor_tensor(m_parts[:, :, 2, :], m_rest[:, :, :], m_parts[:, :, 1, :],
                                      ALU.subtract).then_inc(m_lo_ready, 1)

            heads = ps_ot.rearrange("p g (j c) -> p (g j) c", c=VW)

            def reciprocals(b, q):
                wait(dve, ot_done, b.times(QB, q + 1))
                dve.reciprocal(rden[:, :], heads[:, :, DH]).then_inc(rden_ready, 1)

            def normalise(b, q):
                wait(dve, rden_ready, b.times(QB, q + 1))
                wait(dve, concT_done, b.times(1))
                dve.tensor_tensor(conc[:, q, :, :], heads[:, :, 0:DH],
                                  rden[:, :].unsqueeze(2).broadcast_to([P, H, DH]),
                                  ALU.mult).then_inc(conc_ready, 1)

            def residual(t):
                b = t - 3
                wait(dve, wo_done, b.times(1, 1))
                wait(dve, xb_ready, b.times(1, 1))
                wait(dve, xn2_ready, b.times(1, -1))
                wait(dve, x1_stored[b.mod(2)], b.turn(2, 16))
                dve.tensor_tensor(x1[:, b.mod(2), :, :], ps_shared[:, 0:QB * D].rearrange("p (q d) -> p q d", q=QB),
                                  xb[:, :, :], ALU.add).then_inc(shared_free, 1)

            def stats_out(t):
                b = t - 3
                wait(dve, shared_free, shared_after(t, "wo"))
                wait(dve, mv2_ready, b.times(1))
                norm_stats(x1, stats2, stats2_done, b)

            def step(t):
                a, l, m, e = t + 2, t + 3, t - 1, t - 3
                for h in range(H):
                    if h < 4 and m.on:
                        split_max(t, h)
                    if h in (5, 9) and e.on:
                        reciprocals(e, h // 9)
                    if h in (6, 10) and e.on:
                        normalise(e, h // 10)
                    if h == 14 and a.on:
                        qk_left(t)
                    if h == 7 and l.on:
                        stats_in(t)
                    if h == 8 and l.on:
                        norm_mean_variance(stats1, mv1, mv1_ready, l)
                    if h == 14 and e.on:
                        residual(t)
                    if h == 15 and e.on:
                        stats_out(t)
                    if t.on:
                        row_max(t, h)
                if e.on:
                    norm_mean_variance(stats2, mv2, mv2_ready, e)

            steps(dve, step)


def route_and_share(nc, router_w, shared_fc, shared_proj, xn2T_all, rows, slot_rows, table, out):
    D, NT = xn2T_all.shape[0], rows.shape[1]
    E = router_w.shape[1]
    F = shared_fc.shape[1]
    FC = F // P
    C = 512
    Q = C // P
    CHUNKS = NT // Q
    TILES = table.shape[1]
    TOP_K = 2
    MOST = NT * P // C
    V2 = 2

    with ExitStack() as ctx:
        def sb(name, shape, dt=F32):
            return ctx.enter_context(nc.sbuf_tensor(name, shape, dt))

        def ps(name, shape):
            return ctx.enter_context(nc.psum_tensor(name, shape, F32))

        def sem(name):
            return ctx.enter_context(nc.semaphore(name))

        rw_sb = sb("rw_sb", [D, E])
        fc_sb = sb("fc_sb", [D, F])
        proj_sb = sb("proj_sb", [P, FC, D])
        prob = sb("prob", [P, NT, E])
        chosen = sb("chosen", [P, NT, E])
        chosen_bf = sb("chosen_bf", [P, NT, E], BF16)
        one_number = sb("one_number", [P, NT, 1])
        above = sb("above", [P, NT, E])
        rank = sb("rank", [P, NT, E])
        weight = sb("weight", [P, NT, E])
        choice = [sb(f"choice{r}", [P, NT, E]) for r in range(TOP_K)]
        choice_weight = sb("choice_weight", [P, TOP_K, NT])
        choice_slot = sb("choice_slot", [P, TOP_K, NT])
        choice_row = sb("choice_row", [P, TOP_K, NT], I32)
        before = sb("before", [P, NT, E])
        sums = [sb(f"sums{n}", [P, NT, E]) for n in range(2)]
        slot = sb("slot", [P, NT, E])
        limit_i = sb("limit_i", [P, 1, MOST], I32)
        limit = sb("limit", [P, 1, MOST])
        over = sb("over", [P, E, MOST])
        tiles = sb("tiles", [P, 1, E])
        tiles_sum = sb("tiles_sum", [P, 1, E])
        base = sb("base", [P, 1, E])
        tile_i = sb("tile_i", [P, TILES, 1], I32)
        tile_f = sb("tile_f", [P, TILES, 1])
        ended = sb("ended", [P, TILES, E])
        expert = sb("expert", [P, TILES])
        earlier = sb("earlier", [P, P], BF16)
        ones_bf = sb("ones_bf", [P, P], BF16)
        relu = sb("relu", [P, 2, C])
        hid = sb("hid", [P, 2, FC, C])
        x1c = sb("x1c", [P, 2, Q, D])
        ysum = sb("ysum", [P, 2, Q, D])
        ps_r = ps("ps_r", [P, NT, E])
        ps_before = ps("ps_before", [P, NT, E])
        ps_count = ps("ps_count", [P, NT, E])
        ps_h = [ps(f"ps_h{n}", [P, C]) for n in range(3)]
        ps_y = [ps(f"ps_y{n}", [P, Q, D]) for n in range(2)]

        w_loaded = sem("w_loaded")
        x1_loaded = [sem(f"x1_loaded{n}") for n in range(2)]
        logits_done = sem("logits_done")
        logits_shifted = sem("logits_shifted")
        exp_done = sem("r_exp_done")
        chain = sem("r_chain")
        chosen_ready = sem("chosen_ready")
        counts_done = sem("counts_done")
        consts = sem("r_consts")
        ids_ready = sem("ids_ready")
        first_ready = sem("first_ready")
        first_sent = sem("first_sent")
        second_ready = sem("second_ready")
        second_sent = sem("second_sent")
        h_done = sem("h_done")
        relu_done = sem("relu_done")
        hid_done = sem("hid_done")
        y_done = sem("y_done")
        ysum_ready = sem("ysum_ready")
        stored = [sem(f"y_stored{n}") for n in range(2)]
        block = ctx.enter_context(nc.Block())

        def chunks(eng, step):
            for c in range(V2):
                step(Batch(None, c, CHUNKS, V2))
            with eng.Fori(0, CHUNKS // V2 - 1) as i:
                for c in range(V2, 2 * V2):
                    step(Batch(i, c, CHUNKS, V2))

        def chunk_rows(c):
            return out[bass.ds(c.times(C), C), :].rearrange("(q p) d -> p q d", p=P)

        @block.sync
        def _(sp):
            sp.dma_start(rw_sb[:, :], router_w).then_inc(w_loaded, 16)
            sp.dma_start(fc_sb[:, :], shared_fc).then_inc(w_loaded, 16)
            sp.dma_start(proj_sb[:, :, :], shared_proj.rearrange("(c p) d -> p c d", p=P)).then_inc(w_loaded, 16)

            def load(c):
                wait(sp, ysum_ready, c.times(1, -1))
                sp.dma_start(x1c[:, c.mod(2), :, :], chunk_rows(c)).then_inc(x1_loaded[c.mod(2)], 16)

            def store(c):
                wait(sp, ysum_ready, c.times(1, 1))
                sp.dma_start(chunk_rows(c), ysum[:, c.mod(2), :, :]).then_inc(stored[c.mod(2)], 16)

            for c in range(V2):
                load(Batch(None, c, CHUNKS, V2))
            with sp.Fori(0, CHUNKS // V2 - 1) as i:
                for c in range(V2, 2 * V2):
                    store(Batch(i, c - V2, CHUNKS, V2))
                    load(Batch(i, c, CHUNKS, V2))
            for c in range(CHUNKS - V2, CHUNKS):
                store(Batch(None, c, CHUNKS, V2))
            for n in range(2):
                sp.wait_ge(stored[n], 16 * (CHUNKS // 2))

        @block.gpsimd
        def _(pool):
            pool.memset(earlier[:, :], 1.0).then_inc(consts, 1)
            pool.wait_ge(consts, 1)
            pool.affine_select(out=earlier[:, :], in_=earlier[:, :], compare_op=ALU.is_gt, fill=0.0, base=0,
                               pattern=[[1, P]], channel_multiplier=-1).then_inc(consts, 1)
            pool.memset(ones_bf[:, :], 1.0).then_inc(consts, 1)
            pool.iota(limit_i[:, 0, :], pattern=[[C, MOST]], base=0, channel_multiplier=0).then_inc(consts, 1)
            pool.iota(tile_i[:, :, 0], pattern=[[1, TILES]], base=0, channel_multiplier=0).then_inc(consts, 1)
            pool.iota(rows[:, :, D + 1].bitcast(I32), pattern=[[P, NT]], base=0,
                      channel_multiplier=1).then_inc(ids_ready, 1)
            pool.wait_ge(ids_ready, 1)
            for r, (ready, sent) in enumerate(((first_ready, first_sent), (second_ready, second_sent))):
                pool.wait_ge(ready, 1)
                for t in range(NT):
                    pool.indirect_dma_start(out=slot_rows, out_offset=bass.IndirectOffsetOnAxis(
                        choice_row[:, r, t:t + 1], 0), in_=rows[:, t, :], in_offset=None).then_inc(sent, 16)
            pool.wait_ge(second_sent, 16 * NT)

        @block.tensor
        def _(pe):
            pe.wait_ge(w_loaded, 48)
            for t in range(NT):
                last = pe.matmul(ps_r[:, t, :], xn2T_all[:, t * P:(t + 1) * P], rw_sb[:, :], start=True, stop=True,
                                 skip_group_check=True)
            last.then_inc(logits_done, 1)

            def down(c):
                wait(pe, hid_done, c.times(FC, FC))
                wait(pe, ysum_ready, c.times(1, -1))
                for q in range(Q):
                    for f in range(FC):
                        last = pe.matmul(ps_y[c.mod(2)][:, q, :], hid[:, c.mod(2), f, q * P:(q + 1) * P],
                                         proj_sb[:, f, :], start=f == 0, stop=f == FC - 1, skip_group_check=True)
                last.then_inc(y_done, 1)

            def step(c):
                for f in range(FC):
                    wait(pe, relu_done, c.times(FC, f - 1))
                    pe.matmul(ps_h[f % 2][:, :], fc_sb[:, f * P:(f + 1) * P],
                              xn2T_all[:, bass.ds(c.times(C), C)], start=True, stop=True).then_inc(h_done, 1)
                if c.i is None and c.c == 1:
                    pe.wait_ge(consts, 3)
                    pe.wait_ge(chosen_ready, 1)
                    pe.matmul(ps_before[:, :, :], earlier[:, :], chosen_bf[:, :, :], start=True, stop=True)
                    pe.matmul(ps_count[:, :, :], ones_bf[:, :], chosen_bf[:, :, :], start=True,
                              stop=True).then_inc(counts_done, 1)
                if (c - 1).on:
                    down(c - 1)

            chunks(pe, step)
            down(Batch(None, CHUNKS - 1, CHUNKS, V2))

        @block.scalar
        def _(act):
            act.wait_ge(logits_shifted, 1)
            act.activation(prob[:, :, :], prob[:, :, :], ACT.Exp).then_inc(exp_done, 1)

            def step(c):
                for f in range(FC + 1):
                    if f < FC:
                        wait(act, h_done, c.times(FC, f + 1))
                        wait(act, hid_done, c.times(FC, f - 1))
                        act.activation(relu[:, f % 2, :], ps_h[f % 2][:, :], ACT.Relu).then_inc(relu_done, 1)
                    if f > 0:
                        wait(act, relu_done, c.times(FC, f))
                        if f == 1:
                            wait(act, y_done, c.times(1, -1))
                        act.activation(hid[:, c.mod(2), f - 1, :], relu[:, (f - 1) % 2, :],
                                       ACT.Square).then_inc(hid_done, 1)

            chunks(act, step)

        @block.vector
        def _(dve):
            count = [0]

            def link(ins):
                ins.then_inc(chain, 1)
                count[0] += 1
                dve.wait_ge(chain, count[0])

            def each(a, n=E):
                return a.broadcast_to([P, NT, n])

            dve.wait_ge(logits_done, 1)
            link(dve.tensor_reduce(one_number[:, :, 0], ps_r[:, :, :], AX.X, ALU.max))
            dve.tensor_tensor(prob[:, :, :], ps_r[:, :, :], each(one_number[:, :, :]),
                              ALU.subtract).then_inc(logits_shifted, 1)
            dve.wait_ge(exp_done, 1)
            link(dve.tensor_reduce(one_number[:, :, 0], prob[:, :, :], AX.X, ALU.add))
            link(dve.reciprocal(one_number[:, :, 0], one_number[:, :, 0]))
            link(dve.tensor_tensor(prob[:, :, :], prob[:, :, :], each(one_number[:, :, :]), ALU.mult))
            link(dve.memset(rank[:, :, :], 0.0))
            for e in range(E):
                one = prob[:, :, e:e + 1]
                if e > 0:
                    dve.tensor_tensor(above[:, :, 0:e], each(one, e), prob[:, :, 0:e], ALU.is_gt)
                if e < E - 1:
                    dve.tensor_tensor(above[:, :, e + 1:E], each(one, E - 1 - e), prob[:, :, e + 1:E], ALU.is_ge)
                link(dve.memset(above[:, :, e:e + 1], 0.0))
                link(dve.tensor_tensor(rank[:, :, :], rank[:, :, :], above[:, :, :], ALU.add))
            dve.tensor_scalar(chosen_bf[:, :, :], rank[:, :, :], float(TOP_K), None, ALU.is_lt).then_inc(chosen_ready, 1)
            link(dve.tensor_scalar(chosen[:, :, :], rank[:, :, :], float(TOP_K), None, ALU.is_lt))
            for r in range(TOP_K):
                link(dve.tensor_scalar(choice[r][:, :, :], rank[:, :, :], float(r), None, ALU.is_equal))
            link(dve.tensor_tensor(weight[:, :, :], prob[:, :, :], chosen[:, :, :], ALU.mult))
            link(dve.tensor_reduce(one_number[:, :, 0], weight[:, :, :], AX.X, ALU.add))
            link(dve.tensor_scalar(one_number[:, :, 0], one_number[:, :, 0], 1e-9, None, ALU.max))
            link(dve.reciprocal(one_number[:, :, 0], one_number[:, :, 0]))
            link(dve.tensor_tensor(weight[:, :, :], weight[:, :, :], each(one_number[:, :, :]), ALU.mult))
            for r in range(TOP_K):
                link(dve.tensor_tensor(above[:, :, :], choice[r][:, :, :], weight[:, :, :], ALU.mult))
                link(dve.tensor_reduce(choice_weight[:, r, :], above[:, :, :], AX.X, ALU.add))
            dve.wait_ge(counts_done, 1)
            dve.wait_ge(consts, 5)
            link(dve.tensor_copy(sums[0][:, :, :], ps_count[:, :, :]))
            now, n = 0, 1
            while n < NT:
                a, b = sums[now], sums[1 - now]
                dve.tensor_copy(b[:, 0:n, :], a[:, 0:n, :])
                link(dve.tensor_tensor(b[:, n:NT, :], a[:, n:NT, :], a[:, 0:NT - n, :], ALU.add))
                now, n = 1 - now, 2 * n
            up_to = sums[now]
            link(dve.tensor_copy(limit[:, :, :], limit_i[:, :, :]))
            link(dve.tensor_tensor(over[:, :, :], up_to[:, NT - 1, :].unsqueeze(2).broadcast_to([P, E, MOST]),
                                   limit[:, :, :].broadcast_to([P, E, MOST]), ALU.is_gt))
            link(dve.tensor_reduce(tiles[:, 0, :], over[:, :, :], AX.X, ALU.add))
            link(dve.tensor_copy(tiles_sum[:, :, :], tiles[:, :, :]))
            for e in range(1, E):
                link(dve.tensor_tensor(tiles_sum[:, :, e:e + 1], tiles_sum[:, :, e:e + 1], tiles_sum[:, :, e - 1:e],
                                       ALU.add))
            link(dve.tensor_tensor(base[:, :, :], tiles_sum[:, :, :], tiles[:, :, :], ALU.subtract))
            link(dve.tensor_scalar(base[:, :, :], base[:, :, :], float(C), None, ALU.mult))
            link(dve.tensor_tensor(slot[:, :, :], up_to[:, :, :], ps_count[:, :, :], ALU.subtract))
            link(dve.tensor_tensor(slot[:, :, :], slot[:, :, :], ps_before[:, :, :], ALU.add))
            link(dve.tensor_tensor(slot[:, :, :], slot[:, :, :], base[:, :, :].broadcast_to([P, NT, E]), ALU.add))
            for r in range(TOP_K):
                link(dve.tensor_tensor(above[:, :, :], choice[r][:, :, :], slot[:, :, :], ALU.mult))
                link(dve.tensor_reduce(choice_slot[:, r, :], above[:, :, :], AX.X, ALU.add))
            link(dve.tensor_copy(choice_row[:, :, :], choice_slot[:, :, :]))
            dve.tensor_copy(rows[:, :, D], choice_weight[:, 0, :]).then_inc(first_ready, 1)
            link(dve.tensor_copy(tile_f[:, :, :], tile_i[:, :, :]))
            link(dve.tensor_tensor(ended[:, :, :], tile_f[:, :, :].broadcast_to([P, TILES, E]),
                                   tiles_sum[:, :, :].broadcast_to([P, TILES, E]), ALU.is_ge))
            link(dve.tensor_reduce(expert[:, :], ended[:, :, :], AX.X, ALU.add))
            link(dve.tensor_scalar(expert[:, :], expert[:, :], float(E - 1), None, ALU.min))
            link(dve.tensor_copy(table[:, :], expert[:, :]))

            def step(c):
                wait(dve, y_done, c.times(1, 1))
                wait(dve, x1_loaded[c.mod(2)], c.turn(2, 16, 16))
                wait(dve, stored[c.mod(2)], c.turn(2, 16))
                dve.tensor_tensor(ysum[:, c.mod(2), :, :], ps_y[c.mod(2)][:, :, :], x1c[:, c.mod(2), :, :],
                                  ALU.add).then_inc(ysum_ready, 1)

            chunks(dve, step)
            dve.wait_ge(first_sent, 16 * NT)
            dve.tensor_copy(rows[:, :, D], choice_weight[:, 1, :]).then_inc(second_ready, 1)


def experts(nc, w_fc, w_proj, slot_rows, table, out):
    E, D, F = w_fc.shape
    FC = F // P
    TILES = table.shape[1]
    C = slot_rows.shape[0] // TILES
    Q = C // P
    RW = slot_rows.shape[1]
    V = 3
    TURNS = (TILES - V) // V - 1
    assert TILES % V == 0

    with ExitStack() as ctx:
        def sb(name, shape, dt=F32):
            return ctx.enter_context(nc.sbuf_tensor(name, shape, dt))

        def ps(name, shape):
            return ctx.enter_context(nc.psum_tensor(name, shape, F32))

        def sem(name):
            return ctx.enter_context(nc.semaphore(name))

        ident = sb("ident_e", [P, P])
        fc = sb("fc", [D, V, F])
        proj = sb("proj", [P, V, FC, D])
        tile_rows = sb("tile_rows", [P, V, Q, RW])
        marks = sb("marks", [P, V, Q, 2])
        xT = sb("xT", [D, V, C])
        relu = sb("relu_e", [P, 2, C])
        hid = sb("hid_e", [P, V, FC, C])
        y = sb("y_e", [P, V, Q, D])
        ps_xT = ps("ps_xT", [D, C])
        ps_h = [ps(f"ps_he{n}", [P, C]) for n in range(4)]
        ps_y = [ps(f"ps_ye{n}", [P, Q, D]) for n in range(V)]

        ident_ready = sem("ident_e_ready")
        fc_loaded = [sem(f"fc_loaded{n}") for n in range(V)]
        proj_loaded = [sem(f"proj_loaded{n}") for n in range(V)]
        rows_loaded = [sem(f"rows_loaded{n}") for n in range(V)]
        marks_ready = sem("marks_ready")
        xT_done = sem("xT_done")
        xT_ready = sem("xT_ready")
        h_done = sem("he_done")
        relu_done = sem("relu_e_done")
        hid_done = sem("hid_e_done")
        y_done = sem("ye_done")
        y_ready = sem("y_ready")
        added = [sem(f"added{n}") for n in range(V)]
        block = ctx.enter_context(nc.Block())

        def steps(eng, step, last=TILES):
            for c in range(V):
                step(Batch(None, c, TILES, V))
            with eng.Fori(0, TURNS) as i:
                for c in range(V, 2 * V):
                    step(Batch(i, c, TILES, V))
            for c in range(V + TURNS * V, last + 1):
                step(Batch(None, c, TILES, V))

        @block.sync
        def _(sp):
            def load(b):
                n = b.mod(V)
                e = sp.value_load(table[0:1, bass.ds(b.times(1), 1)], min_val=0, max_val=E - 1)
                wait(sp, marks_ready, b.times(1, -(V - 1)))
                sp.dma_start(tile_rows[:, n, :, :],
                             slot_rows[bass.ds(b.times(C), C), :].rearrange("(q p) d -> p q d", p=P)
                             ).then_inc(rows_loaded[n], 16)
                wait(sp, y_done, b.times(1, -(V - 1)))
                sp.dma_start(fc[:, n, :], w_fc[bass.ds(e, 1), :, :].rearrange("a d f -> (a d) f")).then_inc(fc_loaded[n], 16)
                sp.dma_start(proj[:, n, :, :], w_proj[bass.ds(e, 1), :, :].rearrange("a (c p) d -> p (a c) d", p=P)
                             ).then_inc(proj_loaded[n], 16)

            for c in range(V):
                load(Batch(None, c, TILES, V))
            with sp.Fori(0, TILES // V - 1) as i:
                for c in range(V, 2 * V):
                    load(Batch(i, c, TILES, V))

        @block.gpsimd
        def _(pool):
            pool.memset(ident[:, :], 0.0).then_inc(ident_ready, 1)
            pool.wait_ge(ident_ready, 1)
            pool.affine_select(out=ident[:, :], in_=ident[:, :], compare_op=ALU.not_equal, fill=1.0, base=0,
                               pattern=[[-1, P]], channel_multiplier=1).then_inc(ident_ready, 1)

            def step(b):
                if not b.on:
                    return
                wait(pool, y_ready, b.times(1, 1))
                wait(pool, added[(b - 1).mod(V)], (b - 1).turn(V, 16 * Q, 16 * Q))
                for q in range(Q):
                    pool.indirect_dma_start(
                        out=out, out_offset=bass.IndirectOffsetOnAxis(marks[:, b.mod(V), q, 1:2].bitcast(I32), 0),
                        in_=y[:, b.mod(V), q, :], in_offset=None, compute_op=ALU.add).then_inc(added[b.mod(V)], 16)

            for c in range(TILES):
                step(Batch(None, c, TILES, V))
            for n in range(V):
                pool.wait_ge(added[n], 16 * Q * (TILES // V))

        @block.tensor
        def _(pe):
            pe.wait_ge(ident_ready, 2)

            def turn_rows(b):
                wait(pe, rows_loaded[b.mod(V)], b.turn(V, 16, 16))
                wait(pe, xT_ready, b.times(1))
                for q in range(Q):
                    last = pe.transpose(ps_xT[:, q * P:(q + 1) * P], tile_rows[:, b.mod(V), q, 0:D], ident[:, :])
                last.then_inc(xT_done, 1)

            def up(b):
                wait(pe, fc_loaded[b.mod(V)], b.turn(V, 16, 16))
                wait(pe, xT_ready, b.times(1, 1))
                for f in range(FC):
                    wait(pe, relu_done, b.times(FC, f - 3))
                    pe.matmul(ps_h[f][:, :], fc[:, b.mod(V), f * P:(f + 1) * P], xT[:, b.mod(V), :],
                              start=True, stop=True).then_inc(h_done, 1)

            def down(b):
                wait(pe, proj_loaded[b.mod(V)], b.turn(V, 16, 16))
                wait(pe, hid_done, b.times(FC, FC))
                wait(pe, y_ready, b.times(1, -1))
                for q in range(Q):
                    for f in range(FC):
                        last = pe.matmul(ps_y[b.mod(V)][:, q, :], hid[:, b.mod(V), f, q * P:(q + 1) * P],
                                         proj[:, b.mod(V), f, :], start=f == 0, stop=f == FC - 1,
                                         skip_group_check=True)
                last.then_inc(y_done, 1)

            turn_rows(Batch(None, 0, TILES, V))

            def step(b):
                if b.on:
                    up(b)
                if (b + 1).on:
                    turn_rows(b + 1)
                if (b - 1).on:
                    down(b - 1)

            steps(pe, step)

        @block.scalar
        def _(act):
            def step(b):
                if not b.on:
                    return
                for f in range(FC):
                    wait(act, relu_done, b.times(FC, f + 1))
                    if f == 0:
                        wait(act, y_done, b.times(1, -1))
                    act.activation(hid[:, b.mod(V), f, :], relu[:, f % 2, :], ACT.Square).then_inc(hid_done, 1)

            steps(act, step)

        @block.vector
        def _(dve):
            def rows_turned(b):
                wait(dve, xT_done, b.times(1, 1))
                wait(dve, h_done, b.times(FC, -FC))
                dve.tensor_copy(xT[:, b.mod(V), :], ps_xT[:, :]).then_inc(xT_ready, 1)

            def keep_marks(b):
                wait(dve, rows_loaded[b.mod(V)], b.turn(V, 16, 16))
                wait(dve, added[b.mod(V)], b.turn(V, 16 * Q))
                dve.tensor_copy(marks[:, b.mod(V), :, :], tile_rows[:, b.mod(V), :, D:D + 2]).then_inc(marks_ready, 1)

            def weigh(b):
                wait(dve, y_done, b.times(1, 1))
                wait(dve, marks_ready, b.times(1, 1))
                for q in range(Q):
                    last = dve.tensor_scalar(y[:, b.mod(V), q, :], ps_y[b.mod(V)][:, q, :],
                                             marks[:, b.mod(V), q, 0:1], None, ALU.mult)
                last.then_inc(y_ready, 1)

            rows_turned(Batch(None, 0, TILES, V))

            def step(b):
                if b.on:
                    for f in range(FC):
                        wait(dve, h_done, b.times(FC, f + 1))
                        wait(dve, hid_done, b.times(FC, f - 1))
                        dve.tensor_scalar(relu[:, f % 2, :], ps_h[f][:, :], 0.0, None, ALU.max).then_inc(relu_done, 1)
                if (b + 1).on:
                    rows_turned(b + 1)
                if (b - 1).on:
                    weigh(b - 1)
                if b.on:
                    keep_marks(b)

            steps(dve, step)


_INS = ["x", "wq", "wk", "wv", "wo", "bo", "router_w", "w_fc", "w_proj", "shared_fc", "shared_proj"]


def build(nc, x, wq, wk, wv, wo, bo, router_w, w_fc, w_proj, shared_fc, shared_proj, out):
    B, S, D = x.shape
    E = router_w.shape[1]
    C = out.shape[0] - B * S
    TILES = (2 * B * S - E) // C + E
    with ExitStack() as ctx:
        xn2T_all = ctx.enter_context(nc.sbuf_tensor("xn2T_all", [D, B * S], F32))
        rows = ctx.enter_context(nc.sbuf_tensor("rows", [P, B * S // P, D + 2], F32))
        table = ctx.enter_context(nc.sbuf_tensor("table", [P, TILES], I32))
        slot_rows = nc.dram_tensor("slot_rows", (TILES * C, D + 2), F32, kind="Internal").ap()
        attention(nc, x, wq, wk, wv, wo, bo, xn2T_all, rows, slot_rows, TILES, out)
        route_and_share(nc, router_w, shared_fc, shared_proj, xn2T_all, rows, slot_rows, table, out)
        experts(nc, w_fc, w_proj, slot_rows, table, out)


def kernel(**inputs):
    import numpy as _np
    import concourse.bacc as _bacc
    from concourse import mybir as _mybir
    from concourse.bass_utils import run_bass_kernel_spmd as _run

    a = {k: _np.asarray(v) for k, v in inputs.items()}
    d, heads = a["L0_attn_wq"].shape[0], 16

    def by_depth(w):
        return w.reshape(d, heads, -1).transpose(0, 2, 1).reshape(w.shape)

    laid = {
        "x": a["L0_attn_x"],
        "wq": by_depth(a["L0_attn_wq"]),
        "wk": by_depth(a["L0_attn_wk"]),
        "wv": a["L0_attn_wv"],
        "wo": a["L0_attn_wo"],
        "bo": a["L0_attn_bo"],
        "router_w": a["L0_ffn_router_w"].T,
        "w_fc": a["L0_ffn_w_fc"].transpose(0, 2, 1),
        "w_proj": a["L0_ffn_w_proj"].transpose(0, 2, 1),
        "shared_fc": a["L0_ffn_shared_fc"].T,
        "shared_proj": a["L0_ffn_shared_proj"].T,
    }
    nc = _bacc.Bacc("TRN2", target_bir_lowering=False, num_devices=1)
    arrays, args = {}, []
    for name in _INS:
        v = _np.ascontiguousarray(laid[name])
        arrays[f"in_{name}"] = v
        args.append(nc.dram_tensor(f"in_{name}", v.shape, _mybir.dt.from_np(v.dtype), kind="ExternalInput").ap())
    b, s, _ = a["L0_attn_x"].shape
    out = nc.dram_tensor("out", (b * s + TILE, d), _mybir.dt.float32, kind="ExternalOutput").ap()
    build(nc, *args, out)
    r = _run(nc, [arrays], core_ids=[0])
    return r.results[0]["out"][:b * s].reshape(b, s, d)
```

```python
import concourse.bass as bass
from concourse import mybir
from contextlib import ExitStack

F32 = mybir.dt.float32
BF16 = mybir.dt.bfloat16
F32R = mybir.dt.float32r
I32 = mybir.dt.int32
ALU = mybir.AluOpType
ACT = mybir.ActivationFunctionType
AX = mybir.AxisListType

P = 128
TILE = 512
EPS = 1e-5
U = 4


PRODUCTS = ((0, 0), (0, 1), (1, 0))


class Batch:

    def __init__(self, i, c, total, unroll=U):
        self.i, self.c, self.total, self.unroll = i, c, total, unroll

    def __add__(self, n):
        return Batch(self.i, self.c + n, self.total, self.unroll)

    def __sub__(self, n):
        return self + (-n)

    @property
    def on(self):
        return self.i is not None or 0 <= self.c < self.total

    def mod(self, m):
        return self.c % m

    def times(self, k, n=0):
        return k * self.c + n if self.i is None else self.i * (k * self.unroll) + (k * self.c + n)

    def turn(self, m, k, n=0):
        return k * (self.c // m) + n if self.i is None else self.i * (k * (self.unroll // m)) + (k * (self.c // m) + n)


def wait(eng, sem, value):
    if isinstance(value, int) and value <= 0:
        return
    eng.wait_ge(sem, value)


LOOP_AT = 3 * U


SHARED_USES = [("xnT", 2), ("v", 1), ("mT", -1), ("xn2T", -4), ("concT", -3), ("wo", -3)]


def shared_use(t, name):
    at = [n for n, _ in SHARED_USES].index(name)

    def before(step, upto):
        return sum(0 <= s + d < t.total for s in range(-U, step) for _, d in SHARED_USES) + sum(
            0 <= step + d < t.total for _, d in SHARED_USES[:upto])

    if t.i is None:
        return before(t.c, at)
    return t.i * (U * len(SHARED_USES)) + (before(LOOP_AT, 0) + (t.c - LOOP_AT) * len(SHARED_USES) + at)


def shared_after(t, name):
    return shared_use(t, name) + 1


class ExpertBuffers:

    def __init__(self, ctx, nc, w_fc, w_proj, slot_rows, table, stack_columns):
        self.E, self.D, self.F = w_fc.shape
        self.w_fc, self.w_proj, self.slot_rows, self.table = w_fc, w_proj, slot_rows, table
        self.V = 3
        RW = slot_rows.shape[1]
        self.place = ctx.enter_context(nc.sbuf_tensor("place", [P, stack_columns], F32))
        at = 0

        def part(columns):
            nonlocal at
            at += columns
            assert at <= stack_columns
            return self.place[:, at - columns:at]

        V = self.V
        self.fc = part(V * self.F).rearrange("p (n f) -> p n f", n=V)
        self.proj = part(V * self.F).rearrange("p (n c d) -> p n c d", n=V, d=self.D)
        self.tile_rows = part(V * TILE // P * RW).rearrange("p (n q d) -> p n q d", n=V, d=RW)
        self.fc_loaded = [ctx.enter_context(nc.semaphore(f"fc_loaded{n}")) for n in range(V)]
        self.proj_loaded = [ctx.enter_context(nc.semaphore(f"proj_loaded{n}")) for n in range(V)]
        self.rows_loaded = [ctx.enter_context(nc.semaphore(f"rows_loaded{n}")) for n in range(V)]

    def entry(self, sp, b):
        entry = self.table[0:1, bass.ds(b.times(1), 1), :].rearrange("p t n -> p (t n)")
        return (sp.value_load(entry[:, 0:1], min_val=0, max_val=self.E - 1),
                sp.value_load(entry[:, 1:2], min_val=0, max_val=self.slot_rows.shape[0] - TILE))

    def load_rows(self, sp, b, first):
        n = b.mod(self.V)
        sp.dma_start(self.tile_rows[:, n, :, :],
                     self.slot_rows[bass.ds(first, TILE), :].rearrange("(q p) d -> p q d", p=P)
                     ).then_inc(self.rows_loaded[n], 16)

    def load_weights(self, sp, b, e):
        n = b.mod(self.V)
        sp.dma_start(self.fc[:, n, :], self.w_fc[bass.ds(e, 1), :, :].rearrange("a d f -> (a d) f")
                     ).then_inc(self.fc_loaded[n], 16)
        sp.dma_start(self.proj[:, n, :, :], self.w_proj[bass.ds(e, 1), :, :].rearrange("a (c p) d -> p (a c) d", p=P)
                     ).then_inc(self.proj_loaded[n], 16)


def attention_and_shared(nc, x, wq, wk, wv, wo, bo, router_w, shared_fc, shared_proj, slot_rows, table, ident,
                         expert_buffers, out):
    B, S, D = x.shape
    E = router_w.shape[1]
    H = 16
    DH = D // H
    QB = S // P
    G = H // 4
    OG = G // 2
    VW = 16
    PARTS = 3
    KR = PARTS * PARTS * DH
    KS = 96
    KM = KS + PARTS
    SCALE = float(DH) ** -0.5
    FIRST, LOOPED = -3, LOOP_AT
    TURNS = (B - 4 - LOOPED) // U
    LAST = B + 4
    TOP_K = 2
    GQ = U * QB
    GROUPS = B // U
    LINKS = 29
    LEAVE = 26
    ROOM = (slot_rows.shape[0] - TILE) // E
    TILES = table.shape[1]
    MOST = B * S // TILE
    F = shared_fc.shape[1]
    FC = F // P
    C = 512
    Q = C // P
    CHUNKS = B * S // C
    STORED = 16 * (1 + PARTS)
    STACKED = 16 * (PARTS + 1)

    with ExitStack() as ctx:
        def sb(name, shape, dt=F32):
            return ctx.enter_context(nc.sbuf_tensor(name, shape, dt))

        def ps(name, shape):
            return ctx.enter_context(nc.psum_tensor(name, shape, F32))

        def sem(name):
            return ctx.enter_context(nc.semaphore(name))

        minus_half = sb("minus_half", [P, QB])
        eps_sb = sb("eps_sb", [P, QB])
        wq_sb, wk_sb, wv_sb, wo_sb = (sb(n, [D, D]) for n in ("wq_sb", "wk_sb", "wv_sb", "wo_sb"))
        bo_sb = sb("bo_sb", [P, D])
        router_sb = sb("router_sb", [D, E])
        x_in = sb("x_in", [P, 2, QB, D])
        stats1 = sb("stats1", [P, QB, 6])
        mv1 = sb("mv1", [P, 2, QB, 2])
        centred1 = sb("centred1", [P, QB, D])
        rstd1 = sb("rstd1", [P, QB])
        xn1 = sb("xn1", [P, 2, QB, D])
        xnT = sb("xnT", [D, 2, S])
        qk_parts = sb("qk_parts", [P, 2, PARTS, 2, S], BF16)
        qk_rest = sb("qk_rest", [P, 2, S])
        q_stack = expert_buffers.place[0:KM, :].bitcast(BF16).rearrange("p (n h t) -> p n h t", n=U, h=H)
        k_stack = sb("k_stack", [KM, U, H, S], BF16)
        filler = sb("filler", [P, 2, P], BF16)
        no_rows = sb("no_rows", [P, TILE // P, D + 2])
        ident_bf = sb("ident_bf", [P, P], BF16)
        v_aug = sb("v_aug", [P, U, QB, H // 2, 3, VW])
        neg_max = sb("neg_max", [P, 2, QB, H])
        m_parts = sb("m_parts", [P, QB, P // H, H], BF16)
        m_rest = sb("m_rest", [P, QB, H])
        mT = sb("mT", [PARTS * H, S], BF16)
        probs = sb("probs", [P, 8, QB, S])
        o_sb = sb("o_sb", [P, 2, OG, S])
        rden = sb("rden", [P, QB, H])
        conc = sb("conc", [P, QB, H, DH])
        concT = sb("concT", [D, S])
        x_res = sb("x_res", [P, 2, QB, D])
        xb = sb("xb", [P, QB, D])
        x1 = sb("x1", [P, 2, QB, D])
        xn2T_all = sb("xn2T_all", [D, B * S])
        leaving = sb("leaving", [P, U, QB, TOP_K, D + 2])
        logits = sb("logits", [P, GQ, E])
        prob = sb("prob", [P, GQ, E])
        one_number = sb("one_number", [P, GQ, 1])
        top_prob = sb("top_prob", [P, TOP_K, GQ])
        above = sb("above", [P, GQ, E])
        choice = sb("choice", [P, TOP_K, GQ, E])
        chosen = sb("chosen", [P, GQ, E], BF16)
        weight = sb("weight", [P, TOP_K, GQ])
        counts = sb("counts", [P, GQ + 1, E])
        slot = sb("slot", [P, GQ, E])
        of_choice = sb("of_choice", [P, TOP_K, GQ, E])
        choice_slot = sb("choice_slot", [P, TOP_K, GQ])
        choice_row = sb("choice_row", [P, TOP_K, GQ], I32)
        ids_i = sb("ids_i", [P, GQ], I32)
        ids = sb("ids", [P, GQ])
        next_slot_i = sb("next_slot_i", [P, E], I32)
        next_slot = sb("next_slot", [P, 1, E])
        first_come_i = sb("first_come_i", [P, E], I32)
        first_come = sb("first_come", [P, 1, E])
        limit_i = sb("limit_i", [P, MOST], I32)
        limit = sb("limit", [P, 1, MOST])
        over = sb("over", [P, E, MOST])
        filled = sb("filled", [P, 1, E])
        tiles = sb("tiles", [P, 1, E])
        tiles_sum = sb("tiles_sum", [P, 1, E])
        tile_i = sb("tile_i", [P, TILES], I32)
        tile_f = sb("tile_f", [P, TILES])
        ended = sb("ended", [P, TILES, E])
        passed = sb("passed", [P, TILES, E])
        expert = sb("expert", [P, TILES])
        tile_row = sb("tile_row", [P, TILES])
        room_start = sb("room_start", [P, 1, E])
        tail_row = sb("tail_row", [P, E], I32)
        earlier = sb("earlier", [P, P], BF16)
        ones_bf = sb("ones_bf", [P, P], BF16)
        fc_sb = sb("fc_sb", [D, F])
        sfc_parts = sb("sfc_parts", [D, 2, F], F32R)
        chunk_parts = sb("chunk_parts", [D, 2, 2, C], F32R)
        proj_sb = sb("proj_sb", [P, FC, D])
        relu = sb("relu", [P, 2, C])
        x1c = sb("x1c", [P, 2, Q, D])
        ysum = sb("ysum", [P, 2, Q, D])
        stats2 = sb("stats2", [P, QB, 6])
        mv2 = sb("mv2", [P, 2, QB, 2])
        centred2 = sb("centred2", [P, QB, D])
        rstd2 = sb("rstd2", [P, QB])
        xn2 = sb("xn2", [P, QB, D])
        xn2T = sb("xn2T", [D, S])

        q_dram = nc.dram_tensor("q_parts", (2, PARTS, DH, H, S), BF16, kind="Internal").ap()
        xn2_rows = nc.dram_tensor("xn2_rows", (B * S, D), F32, kind="Internal").ap()
        k_dram = nc.dram_tensor("k_parts", (2, PARTS, PARTS, DH, H, S), BF16, kind="Internal").ap()

        ps_s = [ps(f"ps_s{n}", [P, QB, S]) for n in range(3)]
        ps_st = [ps(f"ps_st{n}", [P, QB, S]) for n in range(2)]
        ps_o = ps("ps_o", [P, 512])
        ps_logits = ps_o[:, S:S + QB * E].rearrange("p (q e) -> p q e", q=QB)
        ps_turn = ps("ps_turn", [P, 512])
        ps_ot = ps_turn[:, :].rearrange("p (q g t) -> p q g t", q=QB, g=OG)
        ps_qk = ps_turn[:, :].rearrange("p (i t) -> p i t", i=2)
        ps_before = ps_o[:, S + QB * E:S + QB * E + GQ * E].rearrange("p (q e) -> p q e", q=GQ)
        ps_all = ps_o[:, S + QB * E + GQ * E:S + QB * E + (GQ + 1) * E]
        ps_counts = ps_o[:, S + QB * E:S + QB * E + (GQ + 1) * E].rearrange("p (q e) -> p q e", e=E)
        hid = probs[:, :, :, :].rearrange("p (n a) q t -> p n (a q t)", n=2).rearrange("p n (f c) -> p n f c", c=C)
        ps_h = [ps_s[n][:, :, :].rearrange("p q t -> p (q t)") for n in range(2)]
        ps_y = [ps_st[n][:, :, :].rearrange("p q (a d) -> p (q a) d", d=D) for n in range(2)]
        ps_shared = ps("ps_shared", [P, 512])
        ps_shared_bf = ps_shared[:, :].bitcast(BF16)

        consts_loaded = sem("consts_loaded")
        consts_ready = sem("consts_ready")
        half_ready = sem("half_ready")
        vpad_ready = sem("vpad_ready")
        rows_filled = sem("rows_filled")
        x_loaded = [sem(f"x_loaded{n}") for n in range(2)]
        stats1_done = sem("stats1_done")
        mv1_ready = sem("mv1_ready")
        rstd1_steps = sem("rstd1_steps")
        xn1_ready = sem("xn1_ready")
        xnT_done = sem("xnT_done")
        qk_done = sem("qk_done")
        qk_hi_ready = sem("qk_hi_ready")
        qk_rest_ready = sem("qk_rest_ready")
        qk_mid_ready = sem("qk_mid_ready")
        qk_lo_ready = sem("qk_lo_ready")
        parts_stored = [sem(f"parts_stored{n}") for n in range(2)]
        v_done = sem("v_done")
        stacked = [sem(f"stacked{n}") for n in range(2)]
        scores_done = sem("scores_done")
        max_done = sem("max_done")
        m_hi_ready = sem("m_hi_ready")
        m_rest_ready = sem("m_rest_ready")
        m_mid_ready = sem("m_mid_ready")
        m_lo_ready = sem("m_lo_ready")
        mT_done = sem("mT_done")
        m_stacked = [sem(f"m_stacked{n}") for n in range(2)]
        scoresT_done = sem("scoresT_done")
        exp_done = sem("exp_done")
        pv_done = sem("pv_done")
        o_ready = sem("o_ready")
        ot_done = sem("ot_done")
        rden_ready = sem("rden_ready")
        conc_ready = sem("conc_ready")
        concT_done = sem("concT_done")
        wo_done = sem("wo_done")
        xres_loaded = [sem(f"xres_loaded{n}") for n in range(2)]
        xb_ready = sem("xb_ready")
        x1_stored = [sem(f"x1_stored{n}") for n in range(2)]
        xn2_stored = [sem(f"xn2_stored{n}") for n in range(2)]
        leaving_loaded = [sem(f"leaving_loaded{n}") for n in range(U)]
        scattered = [sem(f"scattered{n}") for n in range(U)]
        route_ready = sem("route_ready")
        route_consts = sem("route_consts")
        route_links = sem("route_links")
        table_links = sem("table_links")
        table_ready = sem("table_ready")
        logits_exp = sem("logits_exp")
        counts_done = sem("counts_done")
        counts_kept = sem("counts_kept")
        tails_ready = sem("tails_ready")
        shared_loaded = sem("shared_loaded")
        x1_loaded = [sem(f"x1_loaded{n}") for n in range(2)]
        sfc_hi_ready = sem("sfc_hi_ready")
        sfc_ready = sem("sfc_ready")
        chunk_hi_ready = sem("chunk_hi_ready")
        chunk_ready = sem("chunk_ready")
        h_done = sem("h_done")
        relu_done = sem("relu_done")
        hid_done = sem("hid_done")
        y_done = sem("y_done")
        ysum_ready = sem("ysum_ready")
        y_stored = [sem(f"y_stored{n}") for n in range(2)]
        no_rows_ready = sem("no_rows_ready")
        slots_filled = sem("slots_filled")
        stats2_done = sem("stats2_done")
        mv2_ready = sem("mv2_ready")
        rstd2_steps = sem("rstd2_steps")
        xn2_ready = sem("xn2_ready")
        xn2T_done = sem("xn2T_done")
        xn2T_kept = sem("xn2T_kept")
        logits_done = sem("logits_done")
        logits_kept = sem("logits_kept")
        shared_free = sem("shared_free")

        S_BANK = [h % 3 for h in range(H - 1)] + [1]
        S_AGO = [next(n for n in range(1, H) if S_BANK[h - n] == S_BANK[h]) for h in range(H)]

        x_rows = x.rearrange("b s d -> (b s) d")


        def x_batch(row):
            rows = x_rows[bass.ds(row, S), :]
            return rows.rearrange("(q p) d -> p q d", p=P)

        def group_on(t):
            return t.i is not None or 0 <= t.c // U - 2 < GROUPS

        def groups(t, k, n=0):
            return t.turn(U, k, n - 2 * k)

        def chunks(eng, step):
            for c in range(2):
                step(Batch(None, c, CHUNKS, 2))
            with eng.Fori(0, CHUNKS // 2 - 2) as i:
                for c in range(2, 4):
                    step(Batch(i, c, CHUNKS, 2))
            for c in range(CHUNKS - 2, CHUNKS):
                step(Batch(None, c, CHUNKS, 2))

        def chunk_rows(c):
            return out[bass.ds(c.times(C), C), :].rearrange("(q p) d -> p q d", p=P)

        def steps(eng, step, last=LAST):
            for c in range(FIRST, LOOPED):
                step(Batch(None, c, B))
            with eng.Fori(0, TURNS) as i:
                for c in range(LOOPED, LOOPED + U):
                    step(Batch(i, c, B))
            for c in range(LOOPED + U * TURNS, last + 1):
                step(Batch(None, c, B))

        block = ctx.enter_context(nc.Block())

        @block.sync
        def _(sp):
            sp.dma_start(x_in[:, 0, :, :], x_batch(0)).then_inc(x_loaded[0], 16)
            sp.dma_start(x_in[:, 1, :, :], x_batch(S)).then_inc(x_loaded[1], 16)
            for w, src in ((wq_sb, wq), (wk_sb, wk), (wv_sb, wv), (wo_sb, wo), (router_sb, router_w)):
                sp.dma_start(w[:, :], src).then_inc(consts_loaded, 16)
            sp.dma_start(bo_sb[:, :], bo.rearrange("(a n) -> a n", a=1).broadcast_to([P, D])).then_inc(consts_loaded, 16)

            sp.wait_ge(consts_ready, 5)
            for n in range(U):
                for stack in (q_stack, k_stack):
                    sp.dma_start(stack[KR:KS, n, :, :].rearrange("p h t -> p (h t)"),
                                 filler[:, 0:1, :].broadcast_to([P, (KS - KR) * H * S // P // P, P])
                                 ).then_inc(rows_filled, 16)
                sp.dma_start(k_stack[KS:KM, n, :, :].rearrange("p h t -> p (h t)"),
                             filler[0:96, 1:2, :].broadcast_to([96, PARTS * H * S // P // 96, P])
                             ).then_inc(rows_filled, 16)

            for w, src in ((fc_sb[:, :], shared_fc), (proj_sb[:, :, :], shared_proj.rearrange("(c p) d -> p c d", p=P))):
                sp.dma_start(w, src).then_inc(shared_loaded, 16)

            def fill_slots(first):
                sp.dma_start(slot_rows[bass.ds(first, TILE), :].rearrange("(q p) d -> p q d", p=P),
                             no_rows[:, :, :]).then_inc(slots_filled, 16)

            sp.wait_ge(no_rows_ready, 2)
            sp.dma_start(out[B * S:B * S + TILE, :].rearrange("(q p) d -> p q d", p=P),
                         no_rows[:, :, 0:D]).then_inc(slots_filled, 16)
            fill_slots(E * ROOM)

            def load_x(t):
                b = t + 4
                if b.on and not (b.i is None and b.c < 2):
                    wait(sp, xn1_ready, b.times(1, -1))
                    sp.dma_start(x_in[:, b.mod(2), :, :], x_batch(b.times(S))).then_inc(x_loaded[b.mod(2)], 16)

            def load_leaving(t):
                b = t - 9
                if b.on:
                    if b.i is None:
                        wait(sp, xn2_stored[b.mod(2)], b.turn(2, 16, 16))
                    wait(sp, scattered[b.mod(U)], b.turn(U, 16 * QB * TOP_K))
                    for r in range(TOP_K):
                        sp.dma_start(leaving[:, b.mod(U), :, r, 0:D],
                                     xn2_rows[bass.ds(b.times(S), S), :].rearrange("(q p) d -> p q d", p=P)
                                     ).then_inc(leaving_loaded[b.mod(U)], 16)

            def step(t):
                b = t - 2
                if b.on:
                    wait(sp, xb_ready, b.times(1, -1))
                    for q in range(QB):
                        if q == QB - 1 and (t + 1).on:
                            wait(sp, scoresT_done, (t + 1).times(H, -(U - 1) * H))
                        sp.dma_start(x_res[:, b.mod(2), q, :], x_rows[bass.ds(b.times(S, q * P), P), :]
                                     ).then_inc(xres_loaded[b.mod(2)], 16)
                b = t - 4
                if b.on:
                    wait(sp, stats2_done, b.times(1, 1))
                    sp.dma_start(out[bass.ds(b.times(S), S), :].rearrange("(q p) d -> p q d", p=P),
                                 x1[:, b.mod(2), :, :]).then_inc(x1_stored[b.mod(2)], 16)
                    wait(sp, xn2_ready, b.times(1, 1))
                    sp.dma_start(xn2_rows[bass.ds(b.times(S), S), :].rearrange("(q p) d -> p q d", p=P),
                                 xn2[:, :, :]).then_inc(xn2_stored[b.mod(2)], 16)
                load_leaving(t)
                b = t + 1
                if b.on:
                    wait(sp, parts_stored[b.mod(2)], b.turn(2, STORED, STORED))
                    for j in range(PARTS):
                        at = j * PARTS * DH
                        sp.dma_start(q_stack[at:at + PARTS * DH, b.mod(U), :, :],
                                     q_dram[b.mod(2)].rearrange("i d h t -> (i d) h t")
                                     ).then_inc(stacked[b.mod(2)], 16)
                    sp.dma_start(k_stack[0:KR, b.mod(U), :, :],
                                 k_dram[b.mod(2)].rearrange("j i d h t -> (j i d) h t")
                                 ).then_inc(stacked[b.mod(2)], 16)
                load_x(t)
                b = t - 1
                if b.on:
                    wait(sp, shared_free, shared_after(t, "mT"))
                    sp.dma_start(q_stack[KS:KM, b.mod(U), :, :], mT[:, :]).then_inc(m_stacked[b.mod(2)], 16)
                b = t + 2
                if b.on:
                    wait(sp, qk_lo_ready, b.times(1, 1))
                    part = qk_parts[:, b.mod(2), :, :, :]
                    sp.dma_start(q_dram[b.mod(2)].rearrange("i d h t -> (d h) i t"),
                                 part[:, :, 0, :]).then_inc(parts_stored[b.mod(2)], 16)
                    for i in range(PARTS):
                        sp.dma_start(k_dram[b.mod(2), :, i].rearrange("j d h t -> (d h) j t"),
                                     part[:, :, 1, :]).then_inc(parts_stored[b.mod(2)], 16)

            steps(sp, step)
            for n in range(2):
                sp.wait_ge(x1_stored[n], 16 * (B // 2))
            for c in range(LAST + 1, B + 9):
                load_leaving(Batch(None, c, B))

            def load(c):
                wait(sp, ysum_ready, c.times(1, -1))
                sp.dma_start(x1c[:, c.mod(2), :, :], chunk_rows(c)).then_inc(x1_loaded[c.mod(2)], 16)

            def store(c):
                wait(sp, ysum_ready, c.times(1, 1))
                sp.dma_start(chunk_rows(c), ysum[:, c.mod(2), :, :]).then_inc(y_stored[c.mod(2)], 16)

            for c in range(2):
                load(Batch(None, c, CHUNKS, 2))
            sp.wait_ge(tails_ready, 1)
            for e in range(E):
                fill_slots(sp.value_load(tail_row[0:1, e:e + 1], min_val=e * ROOM, max_val=e * ROOM + B * S))
            with sp.Fori(0, CHUNKS // 2 - 1) as i:
                for c in range(2, 4):
                    store(Batch(i, c - 2, CHUNKS, 2))
                    load(Batch(i, c, CHUNKS, 2))
            sp.wait_ge(scoresT_done, B * H)
            sp.wait_ge(table_ready, 1)
            sp.wait_ge(slots_filled, 16 * (2 + E))
            for n in range(U):
                sp.wait_ge(scattered[n], 16 * QB * TOP_K * (B // U))
            for c in range(expert_buffers.V):
                b = Batch(None, c, TILES, expert_buffers.V)
                e, first = expert_buffers.entry(sp, b)
                expert_buffers.load_rows(sp, b, first)
                expert_buffers.load_weights(sp, b, e)
            for c in range(CHUNKS - 2, CHUNKS):
                store(Batch(None, c, CHUNKS, 2))
            for n in range(2):
                sp.wait_ge(y_stored[n], 16 * (CHUNKS // 2))
                sp.wait_ge(xn2_stored[n], 16 * (B // 2))

        @block.gpsimd
        def _(pool):
            pool.memset(ident[:, :], 0.0).then_inc(consts_ready, 1)
            pool.wait_ge(consts_ready, 1)
            pool.affine_select(out=ident[:, :], in_=ident[:, :], compare_op=ALU.not_equal, fill=1.0, base=0,
                               pattern=[[-1, P]], channel_multiplier=1).then_inc(consts_ready, 1)
            pool.wait_ge(consts_ready, 2)
            pool.memset(filler[:, 0, :], 0.0).then_inc(consts_ready, 1)
            pool.memset(filler[:, 1, :], 1.0).then_inc(consts_ready, 1)
            pool.tensor_copy(ident_bf[:, :], ident[:, :]).then_inc(consts_ready, 1)
            pool.memset(no_rows[:, :, :], 0.0).then_inc(no_rows_ready, 1)
            pool.wait_ge(no_rows_ready, 1)
            pool.iota(no_rows[:, :, D + 1].bitcast(I32), pattern=[[P, TILE // P]], base=B * S,
                      channel_multiplier=1).then_inc(no_rows_ready, 1)
            pool.memset(minus_half[:, :], -0.5).then_inc(half_ready, 1)
            pool.memset(eps_sb[:, :], EPS).then_inc(half_ready, 1)
            pool.memset(earlier[:, :], 1.0).then_inc(route_ready, 1)
            pool.wait_ge(route_ready, 1)
            pool.affine_select(out=earlier[:, :], in_=earlier[:, :], compare_op=ALU.is_gt, fill=0.0, base=0,
                               pattern=[[1, P]], channel_multiplier=-1).then_inc(route_ready, 1)
            pool.memset(ones_bf[:, :], 1.0).then_inc(route_ready, 1)
            pool.iota(first_come_i[:, :], pattern=[[-1, E]], base=E, channel_multiplier=0).then_inc(route_ready, 1)
            pool.iota(next_slot_i[:, :], pattern=[[ROOM, E]], base=0, channel_multiplier=0).then_inc(route_ready, 1)
            pool.iota(ids_i[:, :], pattern=[[P, GQ]], base=-GQ * P, channel_multiplier=1).then_inc(route_ready, 1)
            pool.iota(limit_i[:, :], pattern=[[TILE, MOST]], base=0, channel_multiplier=0).then_inc(route_ready, 1)
            pool.iota(tile_i[:, :], pattern=[[1, TILES]], base=0, channel_multiplier=0).then_inc(route_ready, 1)
            pool.wait_ge(half_ready, 2)
            pool.wait_ge(consts_loaded, 16 * 6)

            def normalise(mv, centred, rs, out_, src, chain, b):
                pool.tensor_tensor(rs[:, :], mv[:, b.mod(2), :, 1], eps_sb[:, :], ALU.add).then_inc(chain, 1)
                pool.tensor_tensor(centred[:, :, :], src,
                                   mv[:, b.mod(2), :, 0:1].broadcast_to([P, QB, D]), ALU.subtract).then_inc(chain, 1)
                wait(pool, chain, b.times(3, 1))
                pool.tensor_tensor(rs[:, :], rs[:, :], minus_half[:, :], ALU.pow).then_inc(chain, 1)
                wait(pool, chain, b.times(3, 3))
                return pool.tensor_tensor(out_, centred[:, :, :], rs[:, :].unsqueeze(2).broadcast_to([P, QB, D]),
                                          ALU.mult)

            def rows_leave(t):
                b = t - 12
                if b.on:
                    wait(pool, leaving_loaded[b.mod(U)], b.turn(U, 16 * TOP_K, 16 * TOP_K))
                    wait(pool, route_links, b.turn(U, LINKS, LINKS))

            def scatter(t):
                b = t - 12
                if not b.on:
                    return
                for q in range(QB):
                    for r in range(TOP_K):
                        at = b.mod(U) * QB + q
                        pool.indirect_dma_start(out=slot_rows, out_offset=bass.IndirectOffsetOnAxis(
                            choice_row[:, r, at:at + 1], 0), in_=leaving[:, b.mod(U), q, r, :],
                            in_offset=None).then_inc(scattered[b.mod(U)], 16)

            def step(t):
                rows_leave(t)
                b = t - 3
                if b.on:
                    wait(pool, xres_loaded[b.mod(2)], b.turn(2, 16 * QB, 16 * QB))
                    wait(pool, stats2_done, b.times(1))
                    for q in range(QB):
                        last = pool.tensor_tensor(xb[:, q, :], x_res[:, b.mod(2), q, :], bo_sb[:, :], ALU.add)
                    last.then_inc(xb_ready, 1)
                scatter(t)
                b = t + 3
                if b.on:
                    wait(pool, mv1_ready, b.times(1, 1))
                    wait(pool, xn1_ready, b.times(1))
                    wait(pool, xnT_done, b.times(1, -1))
                    normalise(mv1, centred1, rstd1, xn1[:, b.mod(2), :, :], x_in[:, b.mod(2), :, :],
                              rstd1_steps, b).then_inc(xn1_ready, 1)
                b = t + 2
                if b.on:
                    wait(pool, qk_mid_ready, b.times(1, 1))
                    pool.tensor_tensor(qk_parts[:, b.mod(2), 2, :, :], qk_rest[:, :, :],
                                       qk_parts[:, b.mod(2), 1, :, :], ALU.subtract).then_inc(qk_lo_ready, 1)
                b = t - 3
                if b.on:
                    wait(pool, mv2_ready, b.times(1, 1))
                    wait(pool, xn2_ready, b.times(1))
                    wait(pool, xn2T_done, b.times(1))
                    wait(pool, xn2_stored[(b - 1).mod(2)], (b - 1).turn(2, 16, 16))
                    normalise(mv2, centred2, rstd2, xn2[:, :, :], x1[:, b.mod(2), :, :],
                              rstd2_steps, b).then_inc(xn2_ready, 1)


            steps(pool, step)
            for c in range(LAST + 1, B + 12):
                rows_leave(Batch(None, c, B))
                scatter(Batch(None, c, B))
            for n in range(U):
                pool.wait_ge(scattered[n], 16 * QB * TOP_K * (B // U))

        @block.tensor
        def _(pe):
            pe.wait_ge(consts_ready, 5)
            pe.wait_ge(consts_loaded, 16 * 6)
            pe.wait_ge(vpad_ready, 2)
            pe.wait_ge(route_ready, 8)

            def xnT_use(t):
                b = t + 2
                wait(pe, shared_free, shared_use(t, "xnT"))
                wait(pe, xn1_ready, b.times(1, 1))
                for q in range(QB):
                    last = pe.transpose(ps_shared[:, q * P:(q + 1) * P], xn1[:, b.mod(2), q, :], ident[:, :])
                last.then_inc(xnT_done, 1)

            def project_qk(t):
                b = t + 2
                wait(pe, shared_free, shared_after(t, "xnT"))
                wait(pe, conc_ready, b.times(1, -4))
                pe.matmul(ps_qk[:, 0, :], wq_sb[:, :], xnT[:, b.mod(2), :], start=True, stop=True)
                pe.matmul(ps_qk[:, 1, :], wk_sb[:, :], xnT[:, b.mod(2), :], start=True, stop=True,
                          skip_group_check=True).then_inc(qk_done, 1)

            def project_v(t):
                b = t + 1
                wait(pe, shared_free, shared_use(t, "v"))
                for q in range(QB):
                    last = pe.matmul(ps_shared[:, q * D:(q + 1) * D], xnT[:, b.mod(2), q * P:(q + 1) * P], wv_sb[:, :],
                                     start=True, stop=True, skip_group_check=True)
                last.then_inc(v_done, 1)

            def scores(b, h):
                if h == 0:
                    if b.i is None and b.c == 0:
                        pe.wait_ge(rows_filled, 16 * 3 * U)
                    wait(pe, stacked[b.mod(2)], b.turn(2, STACKED, STACKED))
                wait(pe, max_done, b.times(H, h + 1 - S_AGO[h]))
                for q in range(QB):
                    last = pe.matmul(ps_s[S_BANK[h]][:, q, :], q_stack[0:KS, b.mod(U), h, q * P:(q + 1) * P],
                                     k_stack[0:KS, b.mod(U), h, :], start=True, stop=True, skip_group_check=True)
                last.then_inc(scores_done, 1)

            def maxT(t):
                b = t - 1
                wait(pe, shared_free, shared_use(t, "mT"))
                wait(pe, m_lo_ready, b.times(1, 1))
                for q in range(QB):
                    last = pe.transpose(ps_shared_bf[:, q * P:(q + 1) * P],
                                        m_parts[:, q, :, :].rearrange("p i h -> p (i h)"), ident_bf[:, :])
                last.then_inc(mT_done, 1)

            def scoresT(b, h):
                if h == 0:
                    wait(pe, m_stacked[b.mod(2)], b.turn(2, 16, 16))
                wait(pe, exp_done, b.times(H, h - 1))
                for k in range(QB):
                    last = pe.matmul(ps_st[h % 2][:, k, :], k_stack[0:KM, b.mod(U), h, k * P:(k + 1) * P],
                                     q_stack[0:KM, b.mod(U), h, :], start=True, stop=True, skip_group_check=True)
                last.then_inc(scoresT_done, 1)

            def pv(b, n, k):
                g, second = n // 2, n % 2
                wait(pe, exp_done, b.times(H, 4 * n + 4))
                if not second and k == 0:
                    wait(pe, o_ready, b.times(OG, g))
                for j in range(4):
                    last = pe.matmul(ps_o[32 * j:32 * j + 32, 0:S],
                                     v_aug[:, b.mod(U), k, 4 * g + j, second:second + 2, :].rearrange(
                                         "p a c -> p (a c)"),
                                     probs[:, (4 * n + j) % 8, k, :], start=k == 0 and second == 0,
                                     stop=k == QB - 1 and second == 1, skip_group_check=True)
                if k == QB - 1:
                    last.then_inc(pv_done, 1)

            def oT(b):
                wait(pe, o_ready, b.times(OG, OG))
                wait(pe, qk_rest_ready, b.times(1, 5) if b.i is not None else min(b.c + 5, B))
                for q in range(QB):
                    for g in range(OG):
                        last = pe.transpose(ps_ot[:, q, g, :], o_sb[:, b.mod(2), g, q * P:(q + 1) * P], ident[:, :])
                last.then_inc(ot_done, 1)

            def xn2T_use(t):
                b = t - 4
                wait(pe, shared_free, shared_use(t, "xn2T"))
                wait(pe, xn2_ready, b.times(1, 1))
                for q in range(QB):
                    last = pe.transpose(ps_shared[:, q * P:(q + 1) * P], xn2[:, q, :], ident[:, :])
                last.then_inc(xn2T_done, 1)

            def concT_use(t):
                b = t - 3
                wait(pe, shared_free, shared_use(t, "concT"))
                wait(pe, conc_ready, b.times(1, 1))
                for q in range(QB):
                    last = pe.transpose(ps_shared[:, q * P:(q + 1) * P],
                                        conc[:, q, :, :].rearrange("p h d -> p (h d)"), ident[:, :])
                last.then_inc(concT_done, 1)

            def project_o(t):
                wait(pe, shared_free, shared_after(t, "concT"))
                for q in range(QB):
                    last = pe.matmul(ps_shared[:, q * D:(q + 1) * D], concT[:, q * P:(q + 1) * P], wo_sb[:, :],
                                     start=True, stop=True, skip_group_check=True)
                last.then_inc(wo_done, 1)

            def route(t):
                b = t - 4
                wait(pe, shared_free, shared_after(t, "xn2T"))
                wait(pe, logits_kept, b.times(1))
                if not (t - 2).on:
                    wait(pe, o_ready, OG * B)
                for q in range(QB):
                    last = pe.matmul(ps_logits[:, q, :], xn2T[:, q * P:(q + 1) * P], router_sb[:, :],
                                     start=True, stop=True, skip_group_check=True)
                last.then_inc(logits_done, 1)

            def count(t):
                wait(pe, counts_kept, groups(t, 1))
                wait(pe, route_links, groups(t, LINKS, 17))
                if not (t - 2).on:
                    wait(pe, o_ready, OG * B)
                pe.matmul(ps_before, earlier[:, :], chosen[:, :, :], start=True, stop=False, skip_group_check=True)
                for n in range(1, GQ):
                    pe.matmul(ps_before[:, n:GQ, :], ones_bf[:, :], chosen[:, 0:GQ - n, :], start=False,
                              stop=n == GQ - 1, skip_group_check=True)
                for n in range(GQ):
                    last = pe.matmul(ps_all, ones_bf[:, :], chosen[:, n, :], start=n == 0, stop=n == GQ - 1,
                                     skip_group_check=True)
                last.then_inc(counts_done, 1)

            def step(t):
                l, a, m, c, e, f = t + 2, t + 1, t - 1, t - 2, t - 3, t - 4
                for h in range(H):
                    if h == 0 and l.on:
                        xnT_use(t)
                    if h == 3 and a.on:
                        project_v(t)
                    if h == 12 and l.on:
                        project_qk(t)
                    if h == 5 and m.on:
                        maxT(t)
                    if h == 7 and f.on:
                        xn2T_use(t)
                    if h == 8 and e.on:
                        concT_use(t)
                    if h == 10 and e.on:
                        project_o(t)
                    if t.on:
                        scores(t, h)
                    if c.on:
                        scoresT(c, h)
                    for k in range(QB):
                        if h == 1 + k and e.on:
                            pv(e, G - 1, k)
                        if h - k in (5, 9, 13) and c.on:
                            pv(c, (h - k) // 4 - 1, k)
                    if h == 10 and f.on:
                        route(t)
                    if h == 10 and t.mod(U) == 1 and group_on(t):
                        count(t)
                    if h == 4 and e.on:
                        oT(e)

            steps(pe, step)

            pe.wait_ge(shared_loaded, 32)
            pe.wait_ge(sfc_ready, 1)
            pe.wait_ge(max_done, B * H)
            pe.wait_ge(exp_done, B * H)

            def down(c):
                wait(pe, hid_done, c.times(FC, FC))
                wait(pe, ysum_ready, c.times(1, -1))
                for q in range(Q):
                    for f in range(FC):
                        last = pe.matmul(ps_y[c.mod(2)][:, q, :], hid[:, c.mod(2), f, q * P:(q + 1) * P],
                                         proj_sb[:, f, :], start=f == 0, stop=f == FC - 1, skip_group_check=True)
                last.then_inc(y_done, 1)

            def chunk(c):
                wait(pe, chunk_ready, c.times(1, 1))
                for f in range(FC):
                    wait(pe, relu_done, c.times(FC, f - 1))
                    for n, (w, x) in enumerate(PRODUCTS):
                        last = pe.matmul(ps_h[f % 2], sfc_parts[:, w, f * P:(f + 1) * P],
                                         chunk_parts[:, c.mod(2), x, :], start=n == 0, stop=n == len(PRODUCTS) - 1)
                    last.then_inc(h_done, 1)
                if (c - 1).on:
                    down(c - 1)
                if c.i is None and c.c == 1:
                    count(Batch(None, LAST + 1, B))

            chunks(pe, chunk)
            down(Batch(None, CHUNKS - 1, CHUNKS, 2))

        @block.scalar
        def _(act):
            def xnT_copy(t):
                b = t + 2
                wait(act, xnT_done, b.times(1, 1))
                wait(act, v_done, b.times(1, -1))
                act.activation(xnT[:, b.mod(2), :], ps_shared[:, 0:S], ACT.Copy).then_inc(shared_free, 1)

            def q_hi(t):
                b = t + 2
                wait(act, qk_done, b.times(1, 1))
                wait(act, parts_stored[b.mod(2)], b.turn(2, STORED))
                act.activation(qk_parts[:, b.mod(2), 0, :, :], ps_qk[:, :, :], ACT.Copy).then_inc(qk_hi_ready, 1)

            def v_copy(t):
                b = t + 1
                wait(act, v_done, b.times(1, 1))
                wait(act, pv_done, b.times(G, -(U - 1) * G))
                act.activation(v_aug[:, b.mod(U), :, :, 0:3:2, 0:DH].rearrange("p q h a d -> p (q h) a d"),
                               ps_shared[:, 0:QB * D].rearrange("p (h a d) -> p h a d", a=2, d=DH),
                               ACT.Copy).then_inc(shared_free, 1)

            def exp(b, h):
                wait(act, scoresT_done, b.times(H, h + 1))
                if h % 4 == 0:
                    wait(act, pv_done, b.times(G, h // 4 - 1))
                act.activation(probs[:, h % 8, :, :], ps_st[h % 2][:, :, :], ACT.Exp,
                               scale=SCALE).then_inc(exp_done, 1)

            def o_copy(b, g):
                wait(act, pv_done, b.times(G, 2 * g + 2))
                if g == 0:
                    wait(act, ot_done, b.times(1, -1))
                act.activation(o_sb[:, b.mod(2), g, :], ps_o[:, 0:S], ACT.Copy).then_inc(o_ready, 1)

            def xn2T_copy(t):
                b = t - 4
                wait(act, xn2T_done, b.times(1, 1))
                wait(act, logits_done, b.times(1))
                wait(act, xn2T_kept, b.times(1))
                act.activation(xn2T[:, :], ps_shared[:, 0:S], ACT.Copy).then_inc(shared_free, 1)

            def logits_copy(t):
                b = t - 4
                wait(act, logits_done, b.times(1, 1))
                if b.mod(U) == 0:
                    wait(act, route_links, b.turn(U, LINKS, 2 - LINKS))
                at = b.mod(U) * QB
                act.activation(logits[:, at:at + QB, :], ps_logits, ACT.Copy).then_inc(logits_kept, 1)

            def counts_copy(t):
                wait(act, counts_done, groups(t, 1, 1))
                wait(act, route_links, groups(t, LINKS))
                act.activation(counts[:, :, :], ps_counts, ACT.Copy).then_inc(counts_kept, 1)

            def exp_logits(t):
                wait(act, route_links, groups(t, LINKS, 2))
                act.activation(prob[:, :, :], prob[:, :, :], ACT.Exp).then_inc(logits_exp, 1)

            def keep_xn2T(t):
                b = t - 4
                wait(act, shared_free, shared_after(t, "xn2T"))
                act.activation(xn2T_all[:, bass.ds(b.times(S), S)], xn2T[:, :], ACT.Copy).then_inc(xn2T_kept, 1)

            def concT_copy(t):
                b = t - 3
                wait(act, concT_done, b.times(1, 1))
                act.activation(concT[:, :], ps_shared[:, 0:S], ACT.Copy).then_inc(shared_free, 1)

            def qk_mid(t):
                b = t + 2
                wait(act, qk_rest_ready, b.times(1, 1))
                act.activation(qk_parts[:, b.mod(2), 1, :, :], qk_rest[:, :, :], ACT.Copy).then_inc(qk_mid_ready, 1)

            def mT_copy(t):
                b = t - 1
                wait(act, mT_done, b.times(1, 1))
                wait(act, m_stacked[(b - 1).mod(2)], (b - 1).turn(2, 16, 16))
                act.activation(mT[:, :], ps_shared_bf[0:PARTS * H, 0:S], ACT.Copy).then_inc(shared_free, 1)

            def chunk_high(c):
                if not c.on:
                    return
                wait(act, xn2T_kept, c.times(C // S, C // S))
                wait(act, h_done, c.times(FC, -FC))
                act.activation(chunk_parts[:, c.mod(2), 0, :], xn2T_all[:, bass.ds(c.times(C), C)],
                               ACT.Copy).then_inc(chunk_hi_ready, 1)

            def step(t):
                l, a, m, c, e, f = t + 2, t + 1, t - 1, t - 2, t - 3, t - 4
                if t.i is None and t.c == 1:
                    act.wait_ge(shared_loaded, 32)
                    act.activation(sfc_parts[:, 0, :], fc_sb[:, :], ACT.Copy).then_inc(sfc_hi_ready, 1)
                if t.i is None and t.c == B + 2:
                    for n in range(2):
                        chunk_high(Batch(None, n, CHUNKS, 2))
                for h in range(H):
                    if h == 0 and l.on:
                        xnT_copy(t)
                    if h == 3 and a.on:
                        v_copy(t)
                    if h == 3 and e.on:
                        o_copy(e, OG - 1)
                    if h == 5 and m.on:
                        mT_copy(t)
                    if h == 11 and t.mod(U) == 1 and group_on(t):
                        counts_copy(t)
                    if h == 11 and f.on:
                        logits_copy(t)
                    if h == 11 and c.on:
                        o_copy(c, 0)
                    if h == 7 and f.on:
                        xn2T_copy(t)
                    if h == 8 and e.on:
                        concT_copy(t)
                    if h == 12 and l.on:
                        q_hi(t)
                    if c.on:
                        exp(c, h)
                    if h == 14 and l.on:
                        qk_mid(t)
                    if h == 9 and f.on:
                        keep_xn2T(t)
                    if h == 4 and t.mod(U) == 0 and group_on(t) and not (t.i is None and t.c == LAST):
                        exp_logits(t)

            steps(act, step)

            act.wait_ge(pv_done, B * G)

            def chunk(c):
                for f in range(FC + 1):
                    if f < FC:
                        wait(act, h_done, c.times(FC, f + 1))
                        wait(act, hid_done, c.times(FC, f - 1))
                        act.activation(relu[:, f % 2, :], ps_h[f % 2], ACT.Relu).then_inc(relu_done, 1)
                    if f > 0:
                        wait(act, relu_done, c.times(FC, f))
                        if f == 1:
                            wait(act, y_done, c.times(1, -1))
                        act.activation(hid[:, c.mod(2), f - 1, :], relu[:, (f - 1) % 2, :],
                                       ACT.Square).then_inc(hid_done, 1)
                chunk_high(c + 2)
                if c.i is None and c.c == 0:
                    exp_logits(Batch(None, LAST, B))
                if c.i is None and c.c == 1:
                    counts_copy(Batch(None, LAST + 1, B))

            chunks(act, chunk)

        @block.vector
        def _(dve):
            dve.memset(m_parts[:, :, PARTS:P // H, :], 0.0)
            padded = v_aug[:, :, :, :, :, :].rearrange("p n q h a c -> p (n q h) a c")
            dve.memset(padded[:, :, :, DH:VW], 0.0)
            dve.memset(padded[:, :, 1, 0:DH], 0.0).then_inc(vpad_ready, 1)
            dve.wait_ge(vpad_ready, 1)
            dve.memset(padded[:, :, 0:3:2, DH:DH + 1], 1.0).then_inc(vpad_ready, 1)

            def norm_stats(src, stats, stats_done, b):
                for q in range(QB):
                    last = dve.bn_stats(stats[:, q, :], src[:, b.mod(2), q, :])
                last.then_inc(stats_done, 1)
                wait(dve, stats_done, b.times(1, 1))

            def norm_mean_variance(stats, mv, mv_ready, b):
                for q in range(QB):
                    last = dve.bn_aggr(mv[:, b.mod(2), q, :], stats[:, q, :])
                last.then_inc(mv_ready, 1)

            def stats_in(t):
                b = t + 3
                wait(dve, x_loaded[b.mod(2)], b.turn(2, 16, 16))
                wait(dve, xn1_ready, b.times(1, -1))
                wait(dve, mv1_ready, b.times(1))
                norm_stats(x_in, stats1, stats1_done, b)

            def qk_left(t):
                b = t + 2
                wait(dve, qk_hi_ready, b.times(1, 1))
                wait(dve, qk_lo_ready, b.times(1))
                dve.tensor_tensor(qk_rest[:, :, :], ps_qk[:, :, :], qk_parts[:, b.mod(2), 0, :, :],
                                  ALU.subtract).then_inc(qk_rest_ready, 1)

            def row_max(b, h):
                wait(dve, scores_done, b.times(H, h + 1))
                dve.tensor_reduce(neg_max[:, b.mod(2), :, h], ps_s[S_BANK[h]][:, :, :], AX.X, ALU.max,
                                  negate=True).then_inc(max_done, 1)

            def split_max(t, part):
                b = t - 1
                nm = neg_max[:, b.mod(2), :, :]
                if part == 0:
                    wait(dve, max_done, b.times(H, H))
                    wait(dve, mT_done, b.times(1))
                    dve.tensor_copy(m_parts[:, :, 0, :], nm).then_inc(m_hi_ready, 1)
                elif part == 1:
                    wait(dve, m_hi_ready, b.times(1, 1))
                    dve.tensor_tensor(m_rest[:, :, :], nm, m_parts[:, :, 0, :], ALU.subtract).then_inc(m_rest_ready, 1)
                elif part == 2:
                    wait(dve, m_rest_ready, b.times(1, 1))
                    dve.tensor_copy(m_parts[:, :, 1, :], m_rest[:, :, :]).then_inc(m_mid_ready, 1)
                else:
                    wait(dve, m_mid_ready, b.times(1, 1))
                    dve.tensor_tensor(m_parts[:, :, 2, :], m_rest[:, :, :], m_parts[:, :, 1, :],
                                      ALU.subtract).then_inc(m_lo_ready, 1)

            heads = ps_turn[:, :].rearrange("p (q h c) -> p q h c", q=QB, c=VW)

            def reciprocals(b):
                wait(dve, ot_done, b.times(1, 1))
                dve.reciprocal(rden[:, :, :], heads[:, :, :, DH]).then_inc(rden_ready, 1)

            def normalise(b):
                wait(dve, rden_ready, b.times(1, 1))
                wait(dve, concT_done, b.times(1))
                dve.tensor_tensor(conc[:, :, :, :], heads[:, :, :, 0:DH],
                                  rden[:, :, :].unsqueeze(3).broadcast_to([P, QB, H, DH]),
                                  ALU.mult).then_inc(conc_ready, 1)

            def residual(t):
                b = t - 3
                wait(dve, wo_done, b.times(1, 1))
                wait(dve, xb_ready, b.times(1, 1))
                wait(dve, xn2_ready, b.times(1, -1))
                wait(dve, x1_stored[b.mod(2)], b.turn(2, 16))
                dve.tensor_tensor(x1[:, b.mod(2), :, :], ps_shared[:, 0:QB * D].rearrange("p (q d) -> p q d", q=QB),
                                  xb[:, :, :], ALU.add).then_inc(shared_free, 1)

            def stats_out(t):
                b = t - 3
                wait(dve, shared_free, shared_after(t, "wo"))
                wait(dve, mv2_ready, b.times(1))
                norm_stats(x1, stats2, stats2_done, b)

            def each(a, n=GQ):
                return a.broadcast_to([P, n, E])

            def route(t, n):
                wait(dve, route_links, groups(t, LINKS, n))
                if n == 0:
                    wait(dve, logits_kept, groups(t, U, U))
                    last = dve.tensor_reduce(one_number[:, :, 0], logits[:, :, :], AX.X, ALU.max)
                elif n == 1:
                    last = dve.tensor_tensor(prob[:, :, :], logits[:, :, :], each(one_number[:, :, :]), ALU.subtract)
                elif n == 2:
                    wait(dve, logits_exp, groups(t, 1, 1))
                    last = dve.tensor_reduce(one_number[:, :, 0], prob[:, :, :], AX.X, ALU.add)
                elif n == 3:
                    last = dve.reciprocal(one_number[:, :, 0], one_number[:, :, 0])
                elif n == 4:
                    last = dve.tensor_tensor(prob[:, :, :], prob[:, :, :], each(one_number[:, :, :]), ALU.mult)
                elif n in (5, 11):
                    last = dve.tensor_reduce(top_prob[:, n // 11, :], prob[:, :, :], AX.X, ALU.max)
                elif n in (6, 12):
                    last = dve.tensor_tensor(above[:, :, :], prob[:, :, :],
                                             each(top_prob[:, n // 12, :].unsqueeze(2)), ALU.is_equal)
                elif n in (7, 13):
                    last = dve.tensor_tensor(above[:, :, :], above[:, :, :], each(first_come[:, :, :]), ALU.mult)
                elif n in (8, 14):
                    last = dve.tensor_reduce(one_number[:, :, 0], above[:, :, :], AX.X, ALU.max)
                elif n in (9, 15):
                    last = dve.tensor_tensor(choice[:, n // 15, :, :], each(one_number[:, :, :]),
                                             each(first_come[:, :, :]), ALU.is_equal)
                elif n == 10:
                    last = dve.scalar_tensor_tensor(prob[:, :, :], choice[:, 0, :, :], -2.0, prob[:, :, :],
                                                    ALU.mult, ALU.add)
                elif n == 16:
                    last = dve.tensor_tensor(chosen[:, :, :], choice[:, 0, :, :], choice[:, 1, :, :], ALU.add)
                elif n == 17:
                    last = dve.tensor_tensor(one_number[:, :, 0], top_prob[:, 0, :], top_prob[:, 1, :], ALU.add)
                elif n == 18:
                    last = dve.tensor_scalar(one_number[:, :, 0], one_number[:, :, 0], 1e-9, None, ALU.max)
                elif n == 19:
                    last = dve.reciprocal(one_number[:, :, 0], one_number[:, :, 0])
                elif n == 20:
                    last = dve.tensor_tensor(weight[:, :, :], top_prob[:, :, :],
                                             one_number[:, :, 0].unsqueeze(1).broadcast_to([P, TOP_K, GQ]), ALU.mult)
                elif n == 21:
                    last = dve.tensor_scalar(ids[:, :], ids[:, :], float(GQ * P), None, ALU.add)
                elif n == 22:
                    wait(dve, counts_kept, groups(t, 1, 1))
                    last = dve.tensor_tensor(slot[:, :, :], counts[:, 0:GQ, :], each(next_slot[:, :, :]), ALU.add)
                elif n == 23:
                    last = dve.tensor_tensor(of_choice[:, :, :, :], choice[:, :, :, :],
                                             slot[:, :, :].unsqueeze(1).broadcast_to([P, TOP_K, GQ, E]), ALU.mult)
                elif n == 24:
                    last = dve.tensor_reduce(choice_slot[:, :, :], of_choice[:, :, :, :], AX.X, ALU.add)
                elif n == 25:
                    last = dve.tensor_tensor(next_slot[:, 0, :], next_slot[:, 0, :], counts[:, GQ, :], ALU.add)
                elif n == 26:
                    for j in range(U):
                        wait(dve, scattered[j], groups(t, 16 * QB * TOP_K))
                    last = dve.tensor_copy(choice_row[:, :, :], choice_slot[:, :, :])
                elif n == 27:
                    last = dve.tensor_copy(leaving[:, :, :, :, D], weight[:, :, :].rearrange("p r (j q) -> p j q r", j=U))
                elif n == 28:
                    for r in range(TOP_K):
                        last = dve.tensor_copy(leaving[:, :, :, r, D + 1].bitcast(I32),
                                               ids[:, :].rearrange("p (j q) -> p j q", j=U))
                last.then_inc(route_links, 1)

            def link_at(t, h):
                at = t.mod(U) * H + h
                for first, slots in ((0, range(0, 2)), (2, range(6, 26)), (22, range(32, 36)), (26, range(60, 63))):
                    if at in slots and group_on(t):
                        return first + at - slots[0]
                return None

            def route_constants():
                dve.wait_ge(route_ready, 8)
                dve.tensor_copy(first_come[:, 0, :], first_come_i[:, :]).then_inc(route_consts, 1)
                dve.tensor_copy(next_slot[:, 0, :], next_slot_i[:, :]).then_inc(route_consts, 1)
                dve.tensor_copy(room_start[:, 0, :], next_slot_i[:, :]).then_inc(route_consts, 1)
                dve.tensor_copy(ids[:, :], ids_i[:, :]).then_inc(route_consts, 1)
                dve.tensor_copy(limit[:, 0, :], limit_i[:, :]).then_inc(route_consts, 1)
                dve.tensor_copy(tile_f[:, :], tile_i[:, :]).then_inc(route_consts, 1)
                dve.wait_ge(route_consts, 6)

            def chunk_low(c):
                if not c.on:
                    return
                wait(dve, xn2T_kept, c.times(C // S, C // S))
                wait(dve, chunk_hi_ready, c.times(1, 1))
                dve.tensor_tensor(chunk_parts[:, c.mod(2), 1, :], xn2T_all[:, bass.ds(c.times(C), C)],
                                  chunk_parts[:, c.mod(2), 0, :], ALU.subtract).then_inc(chunk_ready, 1)

            def step(t):
                a, l, m, e = t + 2, t + 3, t - 1, t - 3
                if t.i is None and t.c == 1:
                    route_constants()
                    dve.wait_ge(sfc_hi_ready, 1)
                    dve.tensor_tensor(sfc_parts[:, 1, :], fc_sb[:, :], sfc_parts[:, 0, :],
                                      ALU.subtract).then_inc(sfc_ready, 1)
                if t.i is None and t.c == B + 2:
                    for n in range(2):
                        chunk_low(Batch(None, n, CHUNKS, 2))
                for h in range(H):
                    if link_at(t, h) is not None:
                        route(t, link_at(t, h))
                    if h < 4 and m.on:
                        split_max(t, h)
                    if h == 5 and e.on:
                        reciprocals(e)
                    if h == 6 and e.on:
                        normalise(e)
                    if h == 13 and a.on:
                        qk_left(t)
                    if h == 10 and l.on:
                        stats_in(t)
                    if h == 11 and l.on:
                        norm_mean_variance(stats1, mv1, mv1_ready, l)
                    if h == 11 and e.on:
                        residual(t)
                    if h == 12 and e.on:
                        stats_out(t)
                    if t.on:
                        row_max(t, h)
                if e.on:
                    norm_mean_variance(stats2, mv2, mv2_ready, e)

            steps(dve, step)
            for c in range(LAST + 1, LAST + U):
                for h in range(H):
                    t = Batch(None, c, B)
                    if link_at(t, h) is not None and link_at(t, h) < LEAVE:
                        route(t, link_at(t, h))

            dve.wait_ge(route_links, LINKS * (GROUPS - 1) + LEAVE)
            dve.tensor_copy(tail_row[:, :], next_slot[:, 0, :]).then_inc(tails_ready, 1)

            total = [0]

            def link(ins):
                ins.then_inc(table_links, 1)
                total[0] += 1
                dve.wait_ge(table_links, total[0])

            def table_of_tiles():
                link(dve.tensor_tensor(filled[:, :, :], next_slot[:, :, :], room_start[:, :, :], ALU.subtract))
                link(dve.tensor_tensor(over[:, :, :], filled[:, 0, :].unsqueeze(2).broadcast_to([P, E, MOST]),
                                       limit[:, :, :].broadcast_to([P, E, MOST]), ALU.is_gt))
                link(dve.tensor_reduce(tiles[:, 0, :], over[:, :, :], AX.X, ALU.add))
                link(dve.tensor_copy(tiles_sum[:, :, :], tiles[:, :, :]))
                for e in range(1, E):
                    link(dve.tensor_tensor(tiles_sum[:, :, e:e + 1], tiles_sum[:, :, e:e + 1], tiles_sum[:, :, e - 1:e],
                                           ALU.add))
                link(dve.tensor_tensor(ended[:, :, :], tile_f[:, :].unsqueeze(2).broadcast_to([P, TILES, E]),
                                       each(tiles_sum[:, :, :], TILES), ALU.is_ge))
                link(dve.tensor_reduce(expert[:, :], ended[:, :, :], AX.X, ALU.add))
                link(dve.tensor_tensor(passed[:, :, :], ended[:, :, :], each(tiles[:, :, :], TILES), ALU.mult))
                link(dve.tensor_reduce(tile_row[:, :], passed[:, :, :], AX.X, ALU.add))
                link(dve.tensor_tensor(tile_row[:, :], tile_f[:, :], tile_row[:, :], ALU.subtract))
                link(dve.tensor_scalar(tile_row[:, :], tile_row[:, :], float(TILE), None, ALU.mult))
                link(dve.scalar_tensor_tensor(tile_row[:, :], expert[:, :], float(ROOM), tile_row[:, :], ALU.mult, ALU.add))
                link(dve.tensor_scalar(tile_row[:, :], tile_row[:, :], float(E * ROOM), None, ALU.min))
                link(dve.tensor_scalar(expert[:, :], expert[:, :], float(E - 1), None, ALU.min))
                link(dve.tensor_copy(table[:, :, 0], expert[:, :]))
                dve.tensor_copy(table[:, :, 1], tile_row[:, :]).then_inc(table_ready, 1)

            def chunk(c):
                chunk_low(c + 2)
                wait(dve, y_done, c.times(1, 1))
                wait(dve, x1_loaded[c.mod(2)], c.turn(2, 16, 16))
                wait(dve, y_stored[c.mod(2)], c.turn(2, 16))
                dve.tensor_tensor(ysum[:, c.mod(2), :, :], ps_y[c.mod(2)], x1c[:, c.mod(2), :, :],
                                  ALU.add).then_inc(ysum_ready, 1)
                if c.i is None and c.c == 1:
                    for n in range(LEAVE, LINKS):
                        route(Batch(None, LAST, B), n)
                    table_of_tiles()

            chunks(dve, chunk)


def experts(nc, buffers, ident, out):
    D, F = buffers.D, buffers.F
    FC = F // P
    TILES = buffers.table.shape[1]
    C = TILE
    Q = C // P
    V = buffers.V
    TURNS = (TILES - V) // V - 1
    assert TILES % V == 0

    with ExitStack() as ctx:
        def sb(name, shape, dt=F32):
            return ctx.enter_context(nc.sbuf_tensor(name, shape, dt))

        def ps(name, shape):
            return ctx.enter_context(nc.psum_tensor(name, shape, F32))

        def sem(name):
            return ctx.enter_context(nc.semaphore(name))

        fc, proj, tile_rows = buffers.fc, buffers.proj, buffers.tile_rows
        fc_loaded, proj_loaded, rows_loaded = buffers.fc_loaded, buffers.proj_loaded, buffers.rows_loaded
        marks = sb("marks", [P, V, Q, 2])
        fc_parts = sb("fc_parts", [D, V, 2, F], F32R)
        xT_parts = sb("xT_parts", [D, V, 2, C], F32R)
        relu = sb("relu_e", [P, 2, C])
        hid = sb("hid_e", [P, V, FC, C])
        y = sb("y_e", [P, V, Q, D])
        ps_xT = ps("ps_xT", [D, C])
        ps_h = [ps(f"ps_he{n}", [P, C]) for n in range(4)]
        ps_y = [ps(f"ps_ye{n}", [P, Q, D]) for n in range(V)]

        marks_ready = sem("marks_ready")
        fc_hi_ready = sem("fc_hi_ready")
        fc_ready = sem("fc_ready")
        xT_hi_ready = sem("xT_hi_ready")
        xT_done = sem("xT_done")
        xT_ready = sem("xT_ready")
        h_done = sem("he_done")
        relu_done = sem("relu_e_done")
        hid_done = sem("hid_e_done")
        y_done = sem("ye_done")
        y_ready = sem("y_ready")
        added = [sem(f"added{n}") for n in range(V)]
        block = ctx.enter_context(nc.Block())

        def steps(eng, step, last=TILES):
            for c in range(V):
                step(Batch(None, c, TILES, V))
            with eng.Fori(0, TURNS) as i:
                for c in range(V, 2 * V):
                    step(Batch(i, c, TILES, V))
            for c in range(V + TURNS * V, last + 1):
                step(Batch(None, c, TILES, V))

        @block.sync
        def _(sp):
            def load(b):
                e, first = buffers.entry(sp, b)
                wait(sp, marks_ready, b.times(1, -(V - 1)))
                buffers.load_rows(sp, b, first)
                wait(sp, y_done, b.times(1, -(V - 1)))
                buffers.load_weights(sp, b, e)

            with sp.Fori(0, TILES // V - 1) as i:
                for c in range(V, 2 * V):
                    load(Batch(i, c, TILES, V))

        @block.gpsimd
        def _(pool):
            def step(b):
                if not b.on:
                    return
                wait(pool, y_ready, b.times(1, 1))
                wait(pool, added[(b - 1).mod(V)], (b - 1).turn(V, 16 * Q, 16 * Q))
                for q in range(Q):
                    pool.indirect_dma_start(
                        out=out, out_offset=bass.IndirectOffsetOnAxis(marks[:, b.mod(V), q, 1:2].bitcast(I32), 0),
                        in_=y[:, b.mod(V), q, :], in_offset=None, compute_op=ALU.add).then_inc(added[b.mod(V)], 16)

            for c in range(TILES):
                step(Batch(None, c, TILES, V))
            for n in range(V):
                pool.wait_ge(added[n], 16 * Q * (TILES // V))

        @block.tensor
        def _(pe):
            def turn_rows(b):
                wait(pe, rows_loaded[b.mod(V)], b.turn(V, 16, 16))
                wait(pe, xT_ready, b.times(1))
                for q in range(Q):
                    last = pe.transpose(ps_xT[:, q * P:(q + 1) * P], tile_rows[:, b.mod(V), q, 0:D], ident[:, :])
                last.then_inc(xT_done, 1)

            def up(b):
                wait(pe, fc_ready, b.times(1, 1))
                wait(pe, xT_ready, b.times(1, 1))
                for f in range(FC):
                    wait(pe, relu_done, b.times(FC, f - 3))
                    for n, (w, x) in enumerate(PRODUCTS):
                        last = pe.matmul(ps_h[f][:, :], fc_parts[:, b.mod(V), w, f * P:(f + 1) * P],
                                         xT_parts[:, b.mod(V), x, :], start=n == 0, stop=n == len(PRODUCTS) - 1)
                    last.then_inc(h_done, 1)

            def down(b):
                wait(pe, proj_loaded[b.mod(V)], b.turn(V, 16, 16))
                wait(pe, hid_done, b.times(FC, FC))
                wait(pe, y_ready, b.times(1, -1))
                for q in range(Q):
                    for f in range(FC):
                        last = pe.matmul(ps_y[b.mod(V)][:, q, :], hid[:, b.mod(V), f, q * P:(q + 1) * P],
                                         proj[:, b.mod(V), f, :], start=f == 0, stop=f == FC - 1,
                                         skip_group_check=True)
                last.then_inc(y_done, 1)

            turn_rows(Batch(None, 0, TILES, V))

            def step(b):
                if b.on:
                    up(b)
                if (b + 1).on:
                    turn_rows(b + 1)
                if (b - 1).on:
                    down(b - 1)

            steps(pe, step)

        @block.scalar
        def _(act):
            def high_parts(b):
                wait(act, fc_loaded[b.mod(V)], b.turn(V, 16, 16))
                wait(act, h_done, b.times(FC, -FC * (V - 1)))
                act.activation(fc_parts[:, b.mod(V), 0, :], fc[:, b.mod(V), :], ACT.Copy).then_inc(fc_hi_ready, 1)
                wait(act, xT_done, b.times(1, 1))
                act.activation(xT_parts[:, b.mod(V), 0, :], ps_xT[:, :], ACT.Copy).then_inc(xT_hi_ready, 1)

            high_parts(Batch(None, 0, TILES, V))

            def step(b):
                if not b.on:
                    return
                for f in range(FC):
                    wait(act, relu_done, b.times(FC, f + 1))
                    if f == 0:
                        wait(act, y_done, b.times(1, -1))
                    act.activation(hid[:, b.mod(V), f, :], relu[:, f % 2, :], ACT.Square).then_inc(hid_done, 1)
                if (b + 1).on:
                    high_parts(b + 1)

            steps(act, step)

        @block.vector
        def _(dve):
            def low_parts(b):
                wait(dve, h_done, b.times(FC, -FC * (V - 1)))
                wait(dve, fc_hi_ready, b.times(1, 1))
                dve.tensor_tensor(fc_parts[:, b.mod(V), 1, :], fc[:, b.mod(V), :], fc_parts[:, b.mod(V), 0, :],
                                  ALU.subtract).then_inc(fc_ready, 1)
                wait(dve, xT_hi_ready, b.times(1, 1))
                dve.tensor_tensor(xT_parts[:, b.mod(V), 1, :], ps_xT[:, :], xT_parts[:, b.mod(V), 0, :],
                                  ALU.subtract).then_inc(xT_ready, 1)

            def keep_marks(b):
                wait(dve, rows_loaded[b.mod(V)], b.turn(V, 16, 16))
                wait(dve, added[b.mod(V)], b.turn(V, 16 * Q))
                dve.tensor_copy(marks[:, b.mod(V), :, :], tile_rows[:, b.mod(V), :, D:D + 2]).then_inc(marks_ready, 1)

            def weigh(b):
                wait(dve, y_done, b.times(1, 1))
                wait(dve, marks_ready, b.times(1, 1))
                for q in range(Q):
                    last = dve.tensor_scalar(y[:, b.mod(V), q, :], ps_y[b.mod(V)][:, q, :],
                                             marks[:, b.mod(V), q, 0:1], None, ALU.mult)
                last.then_inc(y_ready, 1)

            low_parts(Batch(None, 0, TILES, V))

            def step(b):
                if b.on:
                    for f in range(FC):
                        wait(dve, h_done, b.times(FC, f + 1))
                        wait(dve, hid_done, b.times(FC, f - 1))
                        dve.tensor_scalar(relu[:, f % 2, :], ps_h[f][:, :], 0.0, None, ALU.max).then_inc(relu_done, 1)
                if (b + 1).on:
                    low_parts(b + 1)
                if (b - 1).on:
                    weigh(b - 1)
                if b.on:
                    keep_marks(b)

            steps(dve, step)


_INS = ["x", "wq", "wk", "wv", "wo", "bo", "router_w", "w_fc", "w_proj", "shared_fc", "shared_proj"]


def build(nc, x, wq, wk, wv, wo, bo, router_w, w_fc, w_proj, shared_fc, shared_proj, out):
    B, S, D = x.shape
    E = router_w.shape[1]
    C = out.shape[0] - B * S
    TILES = (2 * B * S - E) // C + E
    with ExitStack() as ctx:
        table = ctx.enter_context(nc.sbuf_tensor("table", [P, TILES, 2], I32))
        slot_rows = nc.dram_tensor("slot_rows", (E * (B * S + C) + C, D + 2), F32, kind="Internal").ap()
        ident = ctx.enter_context(nc.sbuf_tensor("ident", [P, P], F32))
        buffers = ExpertBuffers(ctx, nc, w_fc, w_proj, slot_rows, table, stack_columns=U * 16 * S // 2)
        attention_and_shared(nc, x, wq, wk, wv, wo, bo, router_w, shared_fc, shared_proj, slot_rows, table, ident,
                             buffers, out)
        experts(nc, buffers, ident, out)


def kernel(**inputs):
    import numpy as _np
    import concourse.bacc as _bacc
    from concourse import mybir as _mybir
    from concourse.bass_utils import run_bass_kernel_spmd as _run

    a = {k: _np.asarray(v) for k, v in inputs.items()}
    d, heads = a["L0_attn_wq"].shape[0], 16

    def by_depth(w):
        return w.reshape(d, heads, -1).transpose(0, 2, 1).reshape(w.shape)

    paired = [8 * g + 4 * second + j for g in range(heads // 8) for j in range(4) for second in range(2)]

    laid = {
        "x": a["L0_attn_x"],
        "wq": by_depth(a["L0_attn_wq"]),
        "wk": by_depth(a["L0_attn_wk"]),
        "wv": a["L0_attn_wv"].reshape(d, heads, -1)[:, paired].reshape(d, d),
        "wo": a["L0_attn_wo"].reshape(heads, -1, d)[paired].reshape(d, d),
        "bo": a["L0_attn_bo"],
        "router_w": a["L0_ffn_router_w"].T,
        "w_fc": a["L0_ffn_w_fc"].transpose(0, 2, 1),
        "w_proj": a["L0_ffn_w_proj"].transpose(0, 2, 1),
        "shared_fc": a["L0_ffn_shared_fc"].T,
        "shared_proj": a["L0_ffn_shared_proj"].T,
    }
    nc = _bacc.Bacc("TRN2", target_bir_lowering=False, num_devices=1)
    arrays, args = {}, []
    for name in _INS:
        v = _np.ascontiguousarray(laid[name])
        arrays[f"in_{name}"] = v
        args.append(nc.dram_tensor(f"in_{name}", v.shape, _mybir.dt.from_np(v.dtype), kind="ExternalInput").ap())
    b, s, _ = a["L0_attn_x"].shape
    out = nc.dram_tensor("out", (b * s + TILE, d), _mybir.dt.float32, kind="ExternalOutput").ap()
    build(nc, *args, out)
    r = _run(nc, [arrays], core_ids=[0])
    return r.results[0]["out"][:b * s].reshape(b, s, d)
```
